# Optimizing a Trainium2 kernel written in Bass

```python
import numpy as np
import jax
import jax.numpy as jnp

def _softmax(x, axis=-1):
    return jax.nn.softmax(x, axis=axis)

def _gelu(x):
    return jax.nn.gelu(x, approximate=True)

def _silu(x):
    return jax.nn.silu(x)

def _sigmoid(x):
    return jax.nn.sigmoid(x)

def _layernorm(x, axis=-1, eps=1e-05):
    m = jnp.mean(x, axis=axis, keepdims=True)
    v = jnp.var(x, axis=axis, keepdims=True)
    return (x - m) / jnp.sqrt(v + eps)

def _scatter_add(tgt, idx, src, axis=0):
    return tgt.at[idx].add(src)

def _segment_sum(src, seg, n):
    return jax.ops.segment_sum(src, seg, n)
kernel_name = 'mk_gnn_preln_d4_gnn_r8_e3da4d'

def setup_inputs(seed: int=0):
    np.random.seed(seed)
    _w = jnp.asarray

    def _rec_inputs():
        import jax
        import jax.numpy as jnp
        _gk = jax.random.key(seed)
        x = -0.0009044 + 1 * jax.random.normal(jax.random.fold_in(_gk, 1), (12500, 16), jnp.float32)
        src = jax.random.randint(jax.random.fold_in(_gk, 2), (400000,), 0, 12500, jnp.int32)
        dst = jax.random.randint(jax.random.fold_in(_gk, 3), (400000,), 0, 12500, jnp.int32)
        _o = jnp.argsort(dst, stable=True)
        src = src[_o]
        dst = dst[_o]
        edge_type_8 = jax.random.randint(jax.random.fold_in(_gk, 12), (400000,), 0, 8, jnp.int32)
        return (x, src, dst, edge_type_8)
    x, src, dst, edge_type_8 = _rec_inputs()

    def _L0_gnn_setup():
        import jax, jax.numpy as jnp
        import numpy as np
        NUM_NODES = 12500
        NUM_EDGES = 200000

        def gcn_conv(x, row, col, W, b, num_nodes):
            loop = jnp.arange(num_nodes)
            row = jnp.concatenate([row, loop])
            col = jnp.concatenate([col, loop])
            h = x @ W
            deg = jax.ops.segment_sum(jnp.ones_like(col, dtype=h.dtype), col, num_segments=num_nodes)
            dinv = jnp.where(deg > 0, jax.lax.rsqrt(deg), 0.0)
            norm = dinv[row] * dinv[col]
            msg = norm[:, None] * h[row]
            out = jax.ops.segment_sum(msg, col, num_segments=num_nodes)
            return out + b
        key = jax.random.key(seed)
        k1, k2, k3, k4 = jax.random.split(key, 4)
        x = jax.random.normal(k1, (NUM_NODES, 16), dtype=jnp.float32)
        edge_index = jax.random.randint(k2, (2, NUM_EDGES), 0, NUM_NODES, dtype=jnp.int64)
        W1 = jax.random.normal(k3, (16, 32), dtype=jnp.float32) * (1.0 / np.sqrt(16))
        b1 = jnp.zeros((32,), dtype=jnp.float32)
        W2 = jax.random.normal(k4, (32, 16), dtype=jnp.float32) * (1.0 / np.sqrt(32))
        b2 = jnp.zeros((16,), dtype=jnp.float32)
        return {'x': x, 'edge_index': edge_index, 'W1': W1, 'b1': b1, 'W2': W2, 'b2': b2}
    _L0_gnn_all = _L0_gnn_setup()
    _L0_gnn_in = {k: v for k, v in _L0_gnn_all.items() if k in ('W1', 'b1', 'W2', 'b2')}
    del _L0_gnn_all

    def _L1_gnn_setup():
        import jax, jax.numpy as jnp
        import numpy as np
        N = 12500
        E = 100000
        F_IN = 16
        H1, C1 = (3, 32)
        H2, C2 = (1, 32)
        NC = 16
        SLOPE = 0.2

        def _gat_layer(x, src, dst, W, a_s, a_d, b, heads, outc):
            h = (x @ W).reshape(N, heads, outc)
            alpha_s = (h * a_s).sum(-1)
            alpha_d = (h * a_d).sum(-1)
            e = jax.nn.leaky_relu(alpha_s[src] + alpha_d[dst], SLOPE)
            m = jax.ops.segment_max(e, dst, num_segments=N)
            p = jnp.exp(e - m[dst])
            z = jax.ops.segment_sum(p, dst, num_segments=N)
            alpha = p / (z[dst] + 1e-16)
            out = jax.ops.segment_sum(h[src] * alpha[:, :, None], dst, num_segments=N)
            return out.reshape(N, heads * outc) + b
        key = jax.random.key(seed)
        ks = jax.random.split(key, 12)
        s = 0.1
        return {'x': jax.random.normal(ks[0], (N, F_IN), jnp.float32), 'edge_index': jax.random.randint(ks[1], (2, E), 0, N, dtype=jnp.int32), 'W1': jax.random.normal(ks[2], (F_IN, H1 * C1), jnp.float32) * s, 'a_src1': jax.random.normal(ks[3], (H1, C1), jnp.float32) * s, 'a_dst1': jax.random.normal(ks[4], (H1, C1), jnp.float32) * s, 'b1': jnp.zeros((H1 * C1,), jnp.float32), 'W2': jax.random.normal(ks[5], (H1 * C1, H2 * C2), jnp.float32) * s, 'a_src2': jax.random.normal(ks[6], (H2, C2), jnp.float32) * s, 'a_dst2': jax.random.normal(ks[7], (H2, C2), jnp.float32) * s, 'b2': jnp.zeros((H2 * C2,), jnp.float32), 'Wf': jax.random.normal(ks[8], (C2, NC), jnp.float32) * s, 'bf': jnp.zeros((NC,), jnp.float32)}
    _L1_gnn_all = _L1_gnn_setup()
    _L1_gnn_in = {k: v for k, v in _L1_gnn_all.items() if k in ('W1', 'a_src1', 'a_dst1', 'b1', 'W2', 'a_src2', 'a_dst2', 'b2', 'Wf', 'bf')}
    del _L1_gnn_all

    def _L2_gnn_setup():
        import jax, jax.numpy as jnp
        import numpy as np
        STALK_DIM = 16
        N_NODES = 6250
        N_EDGES = 50000
        HIDDEN = 64
        key = jax.random.key(seed)
        k1, k2, k3, k4 = jax.random.split(key, 4)
        d = STALK_DIM
        x = jax.random.normal(k1, (N_NODES, d), dtype=jnp.float32)
        edge_index = jax.random.randint(k2, (2, N_EDGES), 0, N_NODES, dtype=jnp.int64)
        W1 = jax.random.normal(k3, (HIDDEN, 2 * d), dtype=jnp.float32) * (1.0 / np.sqrt(2 * d))
        b1 = jnp.zeros((HIDDEN,), dtype=jnp.float32)
        W2 = jax.random.normal(k4, (d, HIDDEN), dtype=jnp.float32) * (1.0 / np.sqrt(HIDDEN))
        b2 = jnp.zeros((d,), dtype=jnp.float32)
        return {'x': x, 'edge_index': edge_index, 'W1': W1, 'b1': b1, 'W2': W2, 'b2': b2}
    _L2_gnn_all = _L2_gnn_setup()
    _L2_gnn_in = {k: v for k, v in _L2_gnn_all.items() if k in ('W1', 'b1', 'W2', 'b2')}
    del _L2_gnn_all

    def _L3_gnn_setup():
        import jax, jax.numpy as jnp
        import numpy as np
        N_NODES = 12500
        N_EDGES = 400000
        NUM_REL = 8

        def _rgcn_layer(x, src, dst, edge_type, W, root, bias):
            out = x @ root + bias
            x_src = x[src]
            for r in range(W.shape[0]):
                mask = (edge_type == r).astype(x.dtype)
                s = jax.ops.segment_sum(x_src * mask[:, None], dst, num_segments=x.shape[0])
                cnt = jax.ops.segment_sum(mask, dst, num_segments=x.shape[0])
                agg = s / jnp.clip(cnt, 1.0)[:, None]
                out = out + agg @ W[r]
            return out
        key = jax.random.key(seed)
        ks = jax.random.split(key, 9)
        x = jax.random.normal(ks[0], (N_NODES, 16), dtype=jnp.float32)
        edge_index = jax.random.randint(ks[1], (2, N_EDGES), 0, N_NODES, dtype=jnp.int32)
        edge_type = jax.random.randint(ks[2], (N_EDGES,), 0, NUM_REL, dtype=jnp.int32)
        s1 = 1.0 / np.sqrt(16.0)
        s2 = 1.0 / np.sqrt(32.0)
        W1 = jax.random.normal(ks[3], (NUM_REL, 16, 32), dtype=jnp.float32) * s1
        root1 = jax.random.normal(ks[4], (16, 32), dtype=jnp.float32) * s1
        b1 = jnp.zeros((32,), dtype=jnp.float32)
        W2 = jax.random.normal(ks[5], (NUM_REL, 32, 16), dtype=jnp.float32) * s2
        root2 = jax.random.normal(ks[6], (32, 16), dtype=jnp.float32) * s2
        b2 = jnp.zeros((16,), dtype=jnp.float32)
        return {'x': x, 'edge_index': edge_index, 'edge_type': edge_type, 'W1': W1, 'root1': root1, 'b1': b1, 'W2': W2, 'root2': root2, 'b2': b2}
    _L3_gnn_all = _L3_gnn_setup()
    _L3_gnn_in = {k: v for k, v in _L3_gnn_all.items() if k in ('W1', 'root1', 'b1', 'W2', 'root2', 'b2')}
    del _L3_gnn_all
    return {'x': x, 'src': src, 'dst': dst, 'edge_type_8': edge_type_8, 'L0_gnn_W1': _L0_gnn_in['W1'], 'L0_gnn_b1': _L0_gnn_in['b1'], 'L0_gnn_W2': _L0_gnn_in['W2'], 'L0_gnn_b2': _L0_gnn_in['b2'], 'L1_gnn_W1': _L1_gnn_in['W1'], 'L1_gnn_a_src1': _L1_gnn_in['a_src1'], 'L1_gnn_a_dst1': _L1_gnn_in['a_dst1'], 'L1_gnn_b1': _L1_gnn_in['b1'], 'L1_gnn_W2': _L1_gnn_in['W2'], 'L1_gnn_a_src2': _L1_gnn_in['a_src2'], 'L1_gnn_a_dst2': _L1_gnn_in['a_dst2'], 'L1_gnn_b2': _L1_gnn_in['b2'], 'L1_gnn_Wf': _L1_gnn_in['Wf'], 'L1_gnn_bf': _L1_gnn_in['bf'], 'L2_gnn_W1': _L2_gnn_in['W1'], 'L2_gnn_b1': _L2_gnn_in['b1'], 'L2_gnn_W2': _L2_gnn_in['W2'], 'L2_gnn_b2': _L2_gnn_in['b2'], 'L3_gnn_W1': _L3_gnn_in['W1'], 'L3_gnn_root1': _L3_gnn_in['root1'], 'L3_gnn_b1': _L3_gnn_in['b1'], 'L3_gnn_W2': _L3_gnn_in['W2'], 'L3_gnn_root2': _L3_gnn_in['root2'], 'L3_gnn_b2': _L3_gnn_in['b2']}

def reference(x, src, dst, edge_type_8, L0_gnn_W1, L0_gnn_b1, L0_gnn_W2, L0_gnn_b2, L1_gnn_W1, L1_gnn_a_src1, L1_gnn_a_dst1, L1_gnn_b1, L1_gnn_W2, L1_gnn_a_src2, L1_gnn_a_dst2, L1_gnn_b2, L1_gnn_Wf, L1_gnn_bf, L2_gnn_W1, L2_gnn_b1, L2_gnn_W2, L2_gnn_b2, L3_gnn_W1, L3_gnn_root1, L3_gnn_b1, L3_gnn_W2, L3_gnn_root2, L3_gnn_b2):
    import jax
    import jax.numpy as jnp

    def _L0_gnn_ref(x, edge_index, W1, b1, W2, b2):
        import jax, jax.numpy as jnp
        import numpy as np
        NUM_NODES = 12500
        NUM_EDGES = 200000

        def gcn_conv(x, row, col, W, b, num_nodes):
            loop = jnp.arange(num_nodes)
            row = jnp.concatenate([row, loop])
            col = jnp.concatenate([col, loop])
            h = x @ W
            deg = jax.ops.segment_sum(jnp.ones_like(col, dtype=h.dtype), col, num_segments=num_nodes)
            dinv = jnp.where(deg > 0, jax.lax.rsqrt(deg), 0.0)
            norm = dinv[row] * dinv[col]
            msg = norm[:, None] * h[row]
            out = jax.ops.segment_sum(msg, col, num_segments=num_nodes)
            return out + b
        row, col = (edge_index[0], edge_index[1])
        h = gcn_conv(x, row, col, W1, b1, NUM_NODES)
        h = jax.nn.relu(h)
        out = gcn_conv(h, row, col, W2, b2, NUM_NODES)
        return out

    def _L1_gnn_ref(x, edge_index, W1, a_src1, a_dst1, b1, W2, a_src2, a_dst2, b2, Wf, bf):
        import jax, jax.numpy as jnp
        import numpy as np
        N = 12500
        E = 100000
        F_IN = 16
        H1, C1 = (3, 32)
        H2, C2 = (1, 32)
        NC = 16
        SLOPE = 0.2

        def _gat_layer(x, src, dst, W, a_s, a_d, b, heads, outc):
            h = (x @ W).reshape(N, heads, outc)
            alpha_s = (h * a_s).sum(-1)
            alpha_d = (h * a_d).sum(-1)
            e = jax.nn.leaky_relu(alpha_s[src] + alpha_d[dst], SLOPE)
            m = jax.ops.segment_max(e, dst, num_segments=N)
            p = jnp.exp(e - m[dst])
            z = jax.ops.segment_sum(p, dst, num_segments=N)
            alpha = p / (z[dst] + 1e-16)
            out = jax.ops.segment_sum(h[src] * alpha[:, :, None], dst, num_segments=N)
            return out.reshape(N, heads * outc) + b
        loops = jnp.arange(N, dtype=edge_index.dtype)
        src = jnp.concatenate([edge_index[0], loops])
        dst = jnp.concatenate([edge_index[1], loops])
        h = jax.nn.selu(_gat_layer(x, src, dst, W1, a_src1, a_dst1, b1, H1, C1))
        h = jax.nn.selu(_gat_layer(h, src, dst, W2, a_src2, a_dst2, b2, H2, C2))
        return h @ Wf + bf

    def _L2_gnn_ref(x, edge_index, W1, b1, W2, b2):
        import jax, jax.numpy as jnp
        import numpy as np
        STALK_DIM = 16
        N_NODES = 6250
        N_EDGES = 50000
        HIDDEN = 64
        d = x.shape[1]
        n = x.shape[0]
        src, dst = (edge_index[0], edge_index[1])
        xs, xd = (x[src], x[dst])

        def reflection(a, b):
            h = jax.nn.relu(jnp.concatenate([a, b], axis=1) @ W1.T + b1)
            return h @ W2.T + b2

        def householder(v):
            vn = v / jnp.maximum(jnp.linalg.norm(v, axis=1, keepdims=True), 1e-12)
            return jnp.eye(d, dtype=v.dtype)[None] - 2.0 * vn[:, :, None] * vn[:, None, :]
        F_s = householder(reflection(xs, xd))
        F_d = householder(reflection(xd, xs))
        L_sd = -jnp.einsum('eki,ekj->eij', F_s, F_d)
        ones_e = jnp.ones(src.shape[0], dtype=x.dtype)
        deg = jnp.zeros(n, dtype=x.dtype).at[src].add(ones_e).at[dst].add(ones_e)
        deg_inv_sqrt = 1.0 / jnp.sqrt(jnp.maximum(deg, 1e-05))
        coef = deg_inv_sqrt[src] * deg_inv_sqrt[dst]
        msg_s = coef[:, None] * jnp.einsum('eij,ej->ei', L_sd, xd)
        msg_d = coef[:, None] * jnp.einsum('eji,ej->ei', L_sd, xs)
        out = x - jnp.zeros_like(x).at[src].add(msg_s) - jnp.zeros_like(x).at[dst].add(msg_d)
        return jax.nn.relu(out)

    def _L3_gnn_ref(x, edge_index, edge_type, W1, root1, b1, W2, root2, b2):
        import jax, jax.numpy as jnp
        import numpy as np
        N_NODES = 12500
        N_EDGES = 400000
        NUM_REL = 8

        def _rgcn_layer(x, src, dst, edge_type, W, root, bias):
            out = x @ root + bias
            x_src = x[src]
            for r in range(W.shape[0]):
                mask = (edge_type == r).astype(x.dtype)
                s = jax.ops.segment_sum(x_src * mask[:, None], dst, num_segments=x.shape[0])
                cnt = jax.ops.segment_sum(mask, dst, num_segments=x.shape[0])
                agg = s / jnp.clip(cnt, 1.0)[:, None]
                out = out + agg @ W[r]
            return out
        src, dst = (edge_index[0], edge_index[1])
        h = _rgcn_layer(x, src, dst, edge_type, W1, root1, b1)
        h = jax.nn.relu(h)
        h = _rgcn_layer(h, src, dst, edge_type, W2, root2, b2)
        return h
    edge_index = jnp.stack([src, dst])
    h = jnp.maximum(_layernorm(x, axis=-1), 0.0)
    x = x + _L0_gnn_ref(h, edge_index, L0_gnn_W1, L0_gnn_b1, L0_gnn_W2, L0_gnn_b2)
    h = jnp.maximum(_layernorm(x, axis=-1), 0.0)
    x = x + _L1_gnn_ref(h, edge_index, L1_gnn_W1, L1_gnn_a_src1, L1_gnn_a_dst1, L1_gnn_b1, L1_gnn_W2, L1_gnn_a_src2, L1_gnn_a_dst2, L1_gnn_b2, L1_gnn_Wf, L1_gnn_bf)
    h = jnp.maximum(_layernorm(x, axis=-1), 0.0)
    x = x + _L2_gnn_ref(h, edge_index, L2_gnn_W1, L2_gnn_b1, L2_gnn_W2, L2_gnn_b2)
    h = jnp.maximum(_layernorm(x, axis=-1), 0.0)
    x = x + _L3_gnn_ref(h, edge_index, edge_type_8, L3_gnn_W1, L3_gnn_root1, L3_gnn_b1, L3_gnn_W2, L3_gnn_root2, L3_gnn_b2)
    return x

_drawn_inputs = setup_inputs


def setup_inputs(seed=0):
    import zlib

    import numpy as np

    out = dict(_drawn_inputs(seed))
    spreads = {'L0_gnn_b1': (0.0, 0.1),
     'L0_gnn_b2': (0.0, 0.1),
     'L1_gnn_b1': (0.0, 0.1),
     'L1_gnn_b2': (0.0, 0.1),
     'L1_gnn_bf': (0.0, 0.1),
     'L2_gnn_b1': (0.0, 0.568),
     'L2_gnn_b2': (0.0, 0.477),
     'L3_gnn_b1': (0.0, 0.1),
     'L3_gnn_b2': (0.0, 0.1)}
    factors = {'L1_gnn_a_src1': 8.0,
     'L1_gnn_a_dst1': 200.0,
     'L1_gnn_a_src2': 200.0,
     'L1_gnn_a_dst2': 200.0}
    for name, (base, spread) in spreads.items():
        noise = np.random.default_rng([zlib.crc32(name.encode()), seed]).standard_normal(out[name].shape)
        drawn = base * np.exp(spread * noise) if base else spread * noise
        out[name] = jnp.asarray(drawn.astype(out[name].dtype))
    for name, factor in factors.items():
        out[name] = (out[name] * factor).astype(out[name].dtype)
    return out
```

```python
import concourse.bass as bass
from concourse import mybir
from contextlib import ExitStack

F32 = mybir.dt.float32
BF16 = mybir.dt.bfloat16
I32 = mybir.dt.int32
ALU = mybir.AluOpType
ACT = mybir.ActivationFunctionType
AX = mybir.AxisListType

P = 128
NODES = 12500
EDGES = 400000
NT = (NODES + P - 1) // P
ROWS = NT * P
COLS = EDGES // P
C = 25
NB = 5
NCH = COLS // C
NIT = NCH // NB
HC = C // NB
G = 7
NG = NT // G
REL = 8
BIG = 1e30
SLOPE = 0.2
EPS = 1e-5
SELU_A = 1.6732632423543772
SELU_S = 1.0507009873554805

GCN1, GCN2, GAT1, GAT2, SHEAF, REL1, REL2 = range(7)
ROW_F = [16, 16, 22, 34, 17, 32, 16]
RUN_W = [24, 16, 54, 34, 16, 32, 16]
SPREAD = {GAT1: 3, GAT2: 1, SHEAF: 17, REL1: 8}
SPREAD_AT = {GAT1: 19, GAT2: 33, SHEAF: 0, REL1: 0}
SPREAD_NO = {GAT1: 0, GAT2: 1, SHEAF: 2, REL1: 3}
HEADS = {GAT1: 3, GAT2: 1}
HEAD_D = {GAT1: 16, GAT2: 32}
T_GCN1, T_GCN2, T_GAT1, T_GAT2, T_SHEAF, T_INV, T_REL1A, T_REL1B, T_REL2 = range(9)
TABLES_BEFORE = [1, 2, 3, 4, 5, 8, 9]
N_LOADS = 33


def build_kernel(nc, A, out):
    ctx = ExitStack()
    with ctx:
        def sb(name, shape, dt=F32):
            return ctx.enter_context(nc.sbuf_tensor(name, shape, dt))

        def sem(name):
            return ctx.enter_context(nc.semaphore(name))

        def dram(name, shape, dt=F32):
            return nc.dram_tensor(name, shape, dt, kind="Internal").ap()

        tables = [dram(f"table{k}", (ROWS, f)) for k, f in enumerate([16, 16, 22, 34, 17])]
        inv_table = dram("inv_table", (ROWS, REL))
        rel1_table = dram("rel1_table", (ROWS * REL, 32))
        rel2_table = dram("rel2_table", (ROWS * REL, 16))
        gathered = tables + [rel1_table, rel2_table]
        running = [dram(f"running{k}", (EDGES, w)) for k, w in enumerate(RUN_W)]
        spread_rows = {k: dram(f"spread{k}", (EDGES + P, n)) for k, n in SPREAD.items()}
        acc_tables = [dram(f"acc{c}", (ROWS + P, 16)) for c in range(C)]

        row_of_src = sb("row_of_src", [P, COLS + NB * C], I32)
        etype = sb("etype", [P, COLS + NB * C], BF16)
        same = sb("same", [P, COLS], BF16)
        weight_lohi = sb("weight_lohi", [P, COLS])
        lohi = weight_lohi[:, :].bitcast(BF16)
        lo_all, hi_all = lohi[:, 0:COLS], lohi[:, COLS:2 * COLS]
        edge_weight = weight_lohi
        x = sb("x", [P, NT, 16])
        hn = sb("hn", [P, NT, 16])
        node_rows = sb("node_rows", [P, NT * 34])
        inv_count = sb("inv_count", [P, NT, REL])
        ends = sb("ends", [P, NT * 54])
        work = sb("work", [P, 13125])
        scratch = sb("scratch", [P, 8192])
        cnt = sb("cnt", [P, NT])
        has = sb("has", [P, NT])
        dinv = sb("dinv", [P, NT])
        dis = sb("dis", [P, NT])
        end_idx = sb("end_idx", [P, NT], I32)
        start_idx = sb("start_idx", [P, NT], I32)
        small = sb("small", [P, 4, NT])
        ident = sb("ident", [P, P])
        ones = sb("ones", [P, P])
        upto = sb("upto", [P, P])
        below = sb("below", [P, P])
        iota_row = sb("iota_row", [P, P])
        iota_bf = sb("iota_bf", [P, P], BF16)
        iota_p = sb("iota_p", [P, 1])
        spare_edge = sb("spare_edge", [P, 1])
        spare_node = sb("spare_node", [P, 1])
        bounds = sb("bounds", [P, 3], I32)
        bnd = sb("bnd", [P, 12])
        first_idx = sb("first_idx", [P, 1], I32)
        first_row = sb("first_row", [P, 34])
        carry = sb("carry", [P, 17])
        onehot_p = sb("onehot_p", [P, P])
        onehot_t = sb("onehot_t", [P, NT])
        not_same_node = sb("not_same_node", [P, P])
        rep = sb("rep", [P, 1])
        tail = sb("tail", [P, 56])
        tail_m = sb("tail_m", [P, 9])
        wide = sb("wide", [P, P])
        idx_chunk = [sb(f"idx_chunk{b}", [P, C], I32) for b in range(NB)]
        add_idx = [sb(f"add_idx{b}", [P, C], I32) for b in range(NB)]
        add_rows = [sb(f"add_rows{b}", [P, C, 16]) for b in range(NB)]
        same_c = sb("same_c", [P, C])
        start_c = sb("start_c", [P, C])
        neg_c = sb("neg_c", [P, C])
        stage = sb("stage", [P, G, 96])
        staged_T = sb("staged_T", [96, G * P])
        w_gcn1 = sb("w_gcn1", [16, 32])
        w_gcn2 = sb("w_gcn2", [32, 16])
        w_gat1 = sb("w_gat1", [16, 96])
        a_gat1 = sb("a_gat1", [16, 2, 96])
        a_gat1w = sb("a_gat1w", [16, 2, 96])
        w_att1 = sb("w_att1", [16, 6])
        w_heads = sb("w_heads", [48, 96])
        w_gat2 = sb("w_gat2", [96, 34])
        a_gat2 = sb("a_gat2", [96, 2, 32])
        w_fin = sb("w_fin", [32, 16])
        w_refl1 = sb("w_refl1", [P, 4, P])
        w_refl2 = sb("w_refl2", [P, 32])
        b_refl1 = sb("b_refl1", [P, 1])
        w_rel1 = sb("w_rel1", [16, REL * 32])
        w_root1 = sb("w_root1", [16, 32])
        w_rel2 = sb("w_rel2", [32, REL * 16])
        w_root2 = sb("w_root2", [32, 16])
        bias = sb("bias", [P, 32 + 16 + 96 + 32 + 16 + 32 + 32 + 16])
        at = [0]

        def bias_at(n):
            at[0] += n
            return bias[:, at[0] - n:at[0]]
        b_gcn1, b_gcn2, b_gat1, b_gat2, b_fin, b_refl2, b_rel1, b_rel2 = [
            bias_at(n) for n in (32, 16, 96, 32, 16, 32, 32, 16)]

        def nodes(tile, f, base=0):
            return tile[:, base:base + NT * f].rearrange("p (t f) -> p t f", f=f)

        rows_at, run_at, spread_at = 0, NB * C * 34, NB * C * (34 + 54)

        def rows_view(b, f):
            o = rows_at + b * C * 34
            return work[:, o:o + C * f].rearrange("p (c f) -> p c f", f=f)

        def run_view(b, w):
            o = run_at + b * C * 54
            return work[:, o:o + C * w].rearrange("p (c f) -> p c f", f=w)

        def spread_view(b, n):
            o = spread_at + b * C * 17
            return work[:, o:o + C * n].rearrange("p (c f) -> p c f", f=n)

        soff = [0]

        def piece(n):
            soff[0] += n
            assert soff[0] <= 8192
            return scratch[:, soff[0] - n:soff[0]]

        hist_onehots = [piece(HC * (P + NT) // 2).bitcast(BF16) for _ in range(NB)]
        hist_lo = [h[:, 0:HC * P].rearrange("p (c n) -> p c n", n=P) for h in hist_onehots]
        hist_hi = [h[:, HC * P:HC * (P + NT)].rearrange("p (c n) -> p c n", n=NT) for h in hist_onehots]
        type_onehot = piece(C * REL).rearrange("p (c r) -> p c r", r=REL)
        soff[0] = 0
        score0 = piece(C * 3)
        score1 = piece(C * 3)
        exp_in = piece(C * 6)
        exp_out = piece(C * 6)
        ratio = piece(C * 3)
        gat_msg = piece(C * 48)
        soff[0] = 0
        rel_onehot = piece(C * REL).rearrange("p (c r) -> p c r", r=REL)
        rel_w = piece(C)
        soff[0] = 0
        pair = piece(C * 32).rearrange("p (c f) -> p c f", f=32)
        pair_T = piece(7 * P)
        hidden = [piece(4 * P) for _ in range(2)]
        refl = piece(C * 32)
        prod = piece(C * 32)
        once = piece(C * 32)
        dots = piece(C * 2)
        inv2 = piece(C * 2)
        equal = [piece(4 * P) for _ in range(2)]
        earlier = piece(4 * P)
        src_f = piece(C)
        rank = piece(C)
        fill_dis = piece(C)
        soff[0] = 0

        ps = [ctx.enter_context(nc.psum_tensor(f"ps{i}", [P, 1024], F32)) for i in range(4)]
        ps_T, ps_Y, ps_hist, ps_misc = ps

        s_loads = sem("s_loads")
        s_zeroed = sem("s_zeroed")
        s_iota = sem("s_iota")
        s_zero_src = sem("s_zero_src")
        s_blk = sem("s_blk")
        s_order = sem("s_order")
        s_hist_ready = [sem(f"s_hist_ready{b}") for b in range(NB)]
        s_hist_used = [sem(f"s_hist_used{b}") for b in range(NB)]
        s_hist_zero = sem("s_hist_zero")
        s_hist_done = sem("s_hist_done")
        s_pe_ask = sem("s_pe_ask")
        s_pe_done = sem("s_pe_done")
        s_act_ask = sem("s_act_ask")
        s_act_done = sem("s_act_done")
        s_rows_stored = sem("s_rows_stored")
        s_rows_ready = sem("s_rows_ready")
        s_idx = [sem(f"s_idx{b}") for b in range(NB)]
        LATER = SHEAF
        s_got_early = [sem(f"s_got_early{b}") for b in range(NB)]
        s_got_later = [sem(f"s_got_later{b}") for b in range(NB)]
        s_run = [sem(f"s_run{b}") for b in range(NB)]
        s_kept = [sem(f"s_kept{b}") for b in range(NB)]
        s_spread_in = [sem(f"s_spread_in{b}") for b in range(NB)]
        s_spread_out = sem("s_spread_out")
        s_first = sem("s_first")
        s_ends = sem("s_ends")
        s_gat_in = sem("s_gat_in")
        s_gat_exp = sem("s_gat_exp")
        s_pair = sem("s_pair")
        s_pair_T = sem("s_pair_T")
        s_pair_S = sem("s_pair_S")
        s_hid = sem("s_hid")
        s_hid_relu = sem("s_hid_relu")
        s_refl = sem("s_refl")
        s_src_row = sem("s_src_row")
        s_msg = sem("s_msg")
        s_src_wide = sem("s_src_wide")
        s_equal = sem("s_equal")
        s_summed = sem("s_summed")
        s_add_ready = [sem(f"s_add_ready{b}") for b in range(NB)]
        s_added = sem("s_added")
        s_lin_in = sem("s_lin_in")
        s_lin_T = sem("s_lin_T")
        s_lin_S = sem("s_lin_S")
        s_lin_out = sem("s_lin_out")
        s_x_in = sem("s_x_in")
        s_x_out = sem("s_x_out")
        s_acc_go = sem("s_acc_go")
        s_acc_in = sem("s_acc_in")
        s_acc_used = sem("s_acc_used")
        s_final = sem("s_final")
        s_out = sem("s_out")

        GROUPS4 = (C + 3) // 4
        N_ZERO = len(SPREAD) + len(acc_tables)
        N_ENDS = 16 * NT
        ACC_ROUND = 5

        def cols_of(g):
            return min(4, C - 4 * g)

        block = ctx.enter_context(nc.Block())

        @block.sync
        def _(sp):
            loads = [0]

            def load(dst, src, slow=False):
                sp.dma_start(dst, src, allow_slow_non_contiguous=slow).then_inc(s_loads, 16)
                loads[0] += 1

            def row(ap):
                return ap.rearrange("(a n) -> a n", a=1)

            dst_pj = A["dst"].rearrange("(p j) -> p j", p=P)
            raw = work[:, :].bitcast(I32)
            load(raw[:, 0:COLS], dst_pj)
            load(bounds[:, 0:1], dst_pj[:, 0:1], slow=True)
            load(bounds[:, 1:2], dst_pj[:, COLS - 1:COLS], slow=True)
            load(bounds[0:P - 1, 2:3], dst_pj[1:P, 0:1], slow=True)
            load(bounds[P - 1:P, 2:3], dst_pj[P - 1:P, COLS - 1:COLS], slow=True)
            load(raw[:, COLS:2 * COLS], A["src"].rearrange("(p j) -> p j", p=P))
            load(raw[:, 2 * COLS:3 * COLS], A["edge_type_8"].rearrange("(p j) -> p j", p=P))
            full = NODES // P
            load(x[:, 0:full, :], A["x"][0:full * P, :].rearrange("(t p) f -> p t f", p=P))
            load(w_gcn1[:, :], A["L0_gnn_W1"])
            load(w_gcn2[:, :], A["L0_gnn_W2"])
            load(w_gat1[:, :], A["L1_gnn_W1"])
            for s, name in enumerate(("L1_gnn_a_src1", "L1_gnn_a_dst1")):
                load(a_gat1[:, s, :], A[name].rearrange("(a h) c -> a (h c)", a=1).partition_broadcast(16))
            load(w_gat2[:, 0:32], A["L1_gnn_W2"])
            for s, name in enumerate(("L1_gnn_a_src2", "L1_gnn_a_dst2")):
                load(a_gat2[:, s, :], A[name].partition_broadcast(96))
            load(w_fin[:, :], A["L1_gnn_Wf"])
            for net in range(2):
                load(b_refl1[64 * net:64 * net + 64, :], A["L2_gnn_b1"].rearrange("(n a) -> n a", a=1))
                load(b_refl2[:, 16 * net:16 * net + 16], row(A["L2_gnn_b2"]).partition_broadcast(P))
            load(w_rel1[:, :], A["L3_gnn_W1"])
            load(w_root1[:, :], A["L3_gnn_root1"])
            load(w_rel2[:, :], A["L3_gnn_W2"])
            load(w_root2[:, :], A["L3_gnn_root2"])
            for tile, name in ((b_gcn1, "L0_gnn_b1"), (b_gcn2, "L0_gnn_b2"), (b_gat1, "L1_gnn_b1"),
                               (b_gat2, "L1_gnn_b2"), (b_fin, "L1_gnn_bf"), (b_rel1, "L3_gnn_b1"),
                               (b_rel2, "L3_gnn_b2")):
                load(tile, row(A[name]).partition_broadcast(P))
            sp.wait_ge(s_zero_src, 1)
            load(x[0:NODES - full * P, full, :], A["x"][full * P:NODES, :])
            assert loads[0] == N_LOADS
            for h in range(3):
                sp.dma_start(w_heads[16 * h:16 * h + 16, 32 * h:32 * h + 32],
                             A["L1_gnn_W1"][:, 32 * h:32 * h + 32]).then_inc(s_blk, 16)
            for net in range(2):
                sp.dma_start(w_refl2[64 * net:64 * net + 64, 16 * net:16 * net + 16],
                             A["L2_gnn_W2"]).then_inc(s_blk, 16)
            for q in range(4):
                for net in range(2):
                    for half in range(2):
                        sp.dma_start(w_refl1[32 * q + 16 * half:32 * q + 16 * half + 16, q, 64 * net:64 * net + 64],
                                     A["L2_gnn_W1"][16 * (half ^ net):16 * (half ^ net) + 16, :]).then_inc(s_blk, 16)
            per_p = (EDGES + P) // P
            zeros = ends[:, 0:per_p]
            for k, n in SPREAD.items():
                sp.dma_start(spread_rows[k].rearrange("(p a) n -> p (a n)", p=P).rearrange("p (n a) -> p n a", a=per_p),
                             zeros.unsqueeze(1).to_broadcast([P, n, per_p])).then_inc(s_zeroed, 16)
            for acc in acc_tables:
                sp.dma_start(acc.rearrange("(p a) f -> p (a f)", p=P), ends[:, 0:(ROWS + P) // P * 16]).then_inc(s_zeroed, 16)
            for b in range(NB):
                sp.sem_inc(s_kept[b], 16)

            def table(n, dst, src):
                sp.wait_ge(s_rows_ready, n + 1)
                sp.dma_start(dst, src).then_inc(s_rows_stored, 16)

            def keep_running(k):
                kept = running[k].rearrange("(p j) w -> p j w", p=P)
                with sp.Fori(0, NIT) as i:
                    for b in range(NB):
                        sp.wait_ge(s_run[b], i + (NIT * k + 1))
                        sp.dma_start(kept[:, bass.ds((i * NB + b) * C, C), :],
                                     run_view(b, RUN_W[k])).then_inc(s_kept[b], 16)

            def whole(t):
                return t.rearrange("(p t) f -> p t f", p=P)

            for k in range(SHEAF + 1):
                table(k, whole(tables[k]), nodes(node_rows, ROW_F[k]))
                keep_running(k)
            for n in range(C // ACC_ROUND):
                if n == 0:
                    sp.wait_ge(s_added, 400 * NCH)
                    for b in range(NB):
                        sp.wait_ge(s_kept[b], 16 * (NIT * (SHEAF + 1) + 1))
                    sp.wait_ge(s_acc_go, 1)
                else:
                    sp.wait_ge(s_acc_used, n)
                for m in range(ACC_ROUND):
                    sp.dma_start(work[:, m * NT * 16:(m + 1) * NT * 16],
                                 acc_tables[n * ACC_ROUND + m][0:ROWS, :].rearrange("(p t) f -> p (t f)", p=P)).then_inc(s_acc_in, 16)
            table(T_INV, whole(inv_table), inv_count[:, :, :])
            rel1 = rel1_table.rearrange("(p t r) f -> p t (r f)", p=P, r=REL)
            for half in range(2):
                table(T_REL1A + half, rel1[:, :, 128 * half:128 * half + 128], nodes(work, P))
            keep_running(REL1)
            table(T_REL2, rel2_table.rearrange("(p t r) f -> p t (r f)", p=P, r=REL), nodes(work, P))
            keep_running(REL2)
            sp.wait_ge(s_final, 1)
            sp.dma_start(out[0:full * P, :].rearrange("(t p) f -> p t f", p=P), x[:, 0:full, :]).then_inc(s_out, 16)
            sp.dma_start(out[full * P:NODES, :], x[0:NODES - full * P, full, :]).then_inc(s_out, 16)
            sp.wait_ge(s_out, 32)

        @block.gpsimd
        def _(pool):
            pool.iota(iota_row[:, :], pattern=[[1, P]], base=0, channel_multiplier=0,
                      allow_small_or_imprecise_dtypes=True).then_inc(s_iota, 1)
            pool.iota(iota_p[:, :], pattern=[[0, 1]], base=0, channel_multiplier=1,
                      allow_small_or_imprecise_dtypes=True).then_inc(s_iota, 1)
            pool.wait_ge(s_zeroed, 16 * N_ZERO)

            def fetch_chunk(k, b, turn):
                pool.wait_ge(s_idx[b], turn + ((NIT + 1) * k + 1))
                pool.nop(nofuse=True)
                rows = rows_view(b, ROW_F[k])
                for c in range(C):
                    pool.indirect_dma_start(rows[:, c, :], None, gathered[k],
                                            bass.IndirectOffsetOnAxis(ap=idx_chunk[b][:, c:c + 1], axis=0)).then_inc((s_got_early if k < LATER else s_got_later)[b], 16)

            def add_chunk(b, turn):
                pool.wait_ge(s_add_ready[b], turn + 1)
                pool.nop(nofuse=True)
                for c in range(C):
                    pool.indirect_dma_start(acc_tables[c], bass.IndirectOffsetOnAxis(ap=add_idx[b][:, c:c + 1], axis=0),
                                            add_rows[b][:, c, :], None, compute_op=ALU.add).then_inc(s_added, 16)

            def scatter_spread(k):
                n = SPREAD[k]
                src = inv_count[:, :, :] if k == REL1 else nodes(node_rows, ROW_F[k])
                at_lane = SPREAD_AT[k]
                for t in range(NT):
                    pool.indirect_dma_start(spread_rows[k], bass.IndirectOffsetOnAxis(ap=start_idx[:, t:t + 1], axis=0),
                                            src[:, t, at_lane:at_lane + n], None).then_inc(s_spread_out, 16)

            for k in range(7):
                if k in SPREAD:
                    pool.wait_ge(s_rows_ready, TABLES_BEFORE[k])
                    scatter_spread(k)
                pool.wait_ge(s_rows_stored, 16 * TABLES_BEFORE[k])
                if k in SPREAD:
                    table = inv_table if k == REL1 else tables[k]
                    width = REL if k == REL1 else ROW_F[k]
                    pool.indirect_dma_start(first_row[:, 0:width], None, table,
                                            bass.IndirectOffsetOnAxis(ap=first_idx[:, 0:1], axis=0)).then_inc(s_first, 16)
                if k != SHEAF:
                    with pool.Fori(0, NIT) as i:
                        for b in range(NB):
                            fetch_chunk(k, b, i)
                else:
                    AHEAD = 3
                    for b in range(AHEAD):
                        fetch_chunk(k, b, 0)
                    with pool.Fori(0, NIT - 1) as i:
                        for b in range(NB):
                            add_chunk(b, i)
                            fetch_chunk(k, (b + AHEAD) % NB, i + (b + AHEAD) // NB)
                            pool.wait_ge(s_added, (i * NB + (b + 1)) * 400)
                    for b in range(NB):
                        add_chunk(b, NIT - 1)
                        if b + AHEAD < NB:
                            fetch_chunk(k, b + AHEAD, NIT - 1)
                        pool.wait_ge(s_added, 400 * (NB * (NIT - 1) + b + 1))
                for b in range(NB):
                    pool.wait_ge(s_kept[b], 16 * (NIT * (k + 1) + 1))
                w = RUN_W[k]
                for t in range(NT):
                    pool.indirect_dma_start(nodes(ends, w)[:, t, :], None, running[k],
                                            bass.IndirectOffsetOnAxis(ap=end_idx[:, t:t + 1], axis=0)).then_inc(s_ends, 16)

        @block.scalar
        def _(act):
            asked = [0]
            lin = [0]

            def node_function(dst, src, func):
                asked[0] += 1
                act.wait_ge(s_act_ask, asked[0])
                nc.scalar.activation(dst, src, func).then_inc(s_act_done, 1)

            def linear(fi):
                base = NG * lin[0]
                lin[0] += 1
                with act.Fori(0, NG) as g:
                    act.wait_ge(s_lin_T, g + (base + 1))
                    nc.scalar.activation(staged_T[0:fi, :], ps_T[0:fi, 0:G * P], ACT.Copy).then_inc(s_lin_S, 1)

            def load_spread(k, b, i):
                e = SPREAD_NO[k]
                act.wait_ge(s_idx[b], i + ((NIT + 1) * k + 1))
                act.dma_start(spread_view(b, SPREAD[k]),
                              spread_rows[k][0:EDGES, :].rearrange("(p j) n -> p j n", p=P)[:, bass.ds((i * NB + b) * C, C), :]
                              ).then_inc(s_spread_in[b], 16)

            def spread_landed(k):
                act.wait_ge(s_spread_out, N_ENDS * (SPREAD_NO[k] + 1))

            def gat_pass(k):
                spread_landed(k)
                n = 2 * HEADS[k] * C
                with act.Fori(0, NIT) as i:
                    for b in range(NB):
                        load_spread(k, b, i)
                        act.wait_ge(s_gat_in, (i * NB + b) + (NCH * (k - GAT1) + 1))
                        nc.scalar.activation(exp_out[:, 0:n], exp_in[:, 0:n], ACT.Exp).then_inc(s_gat_exp, 1)

            def sheaf_pass():
                spread_landed(SHEAF)
                with act.Fori(0, NIT) as i:
                    for b in range(NB):
                        c = i * NB + b
                        load_spread(SHEAF, b, i)
                        act.wait_ge(s_pair_T, c + 1)
                        nc.scalar.activation(pair_T[:, 0:6 * P], ps_T[:, 0:6 * P], ACT.Copy)
                        nc.scalar.activation(pair_T[0:32, 6 * P:7 * P], ps_T[0:32, 6 * P:7 * P], ACT.Copy).then_inc(s_pair_S, 1)
                        for g in range(GROUPS4):
                            n = cols_of(g) * P
                            act.wait_ge(s_hid, c * GROUPS4 + (g + 1))
                            if g >= 2:
                                act.wait_ge(s_refl, c * GROUPS4 + (g - 1))
                            nc.scalar.activation(hidden[g % 2][:, 0:n], ps_hist[:, 512 * (g % 2):512 * (g % 2) + n],
                                                 ACT.Relu, bias=b_refl1[:, 0:1]).then_inc(s_hid_relu, 1)

            node_function(small[:, 1, :], small[:, 0, :], ACT.Sqrt)
            node_function(small[:, 1, :], small[:, 0, :], ACT.Sqrt)
            linear(16)
            linear(32)
            node_function(small[:, 1, :], small[:, 0, :], ACT.Sqrt)
            linear(16)
            gat_pass(GAT1)
            node_function(tail_m[:, 3:6], tail_m[:, 3:6], ACT.Exp)
            merge = work[:, 9408:9408 + 9 * NT]
            node_function(merge, merge, ACT.Exp)
            linear(48)
            for _ in range(2):
                node_function(scratch[:, 0:48 * NT], scratch[:, 0:48 * NT], ACT.Exp)
            linear(96)
            gat_pass(GAT2)
            node_function(tail_m[:, 3:4], tail_m[:, 3:4], ACT.Exp)
            merge = work[:, 9408:9408 + 3 * NT]
            node_function(merge, merge, ACT.Exp)
            node_function(scratch[:, 0:32 * NT], scratch[:, 0:32 * NT], ACT.Exp)
            linear(32)
            node_function(small[:, 1, :], small[:, 0, :], ACT.Sqrt)
            node_function(small[:, 1, :], small[:, 0, :], ACT.Sqrt)
            sheaf_pass()
            node_function(small[:, 1, :], small[:, 0, :], ACT.Sqrt)
            linear(16)
            linear(16)
            linear(16)
            spread_landed(REL1)
            with act.Fori(0, NIT) as i:
                for b in range(NB):
                    load_spread(REL1, b, i)
            linear(32)
            linear(32)

        @block.tensor
        def _(pe):
            asked = [0]
            lin = [0]
            xtr = [0]
            zero_bf = scratch[:, 8000:8128].bitcast(BF16)

            def count(kh):
                pe.wait_ge(s_hist_zero, kh + 1)
                nc.tensor.matmul(ps_hist[:, 0:NT], zero_bf[:, 0:P], zero_bf[:, 0:NT], start=True, stop=False, skip_group_check=True)
                with pe.Fori(0, NCH) as i:
                    for b in range(NB):
                        pe.wait_ge(s_hist_ready[b], i + (NCH * kh + 1))
                        for c in range(HC):
                            last = nc.tensor.matmul(ps_hist[:, 0:NT], hist_lo[b][:, c, :], hist_hi[b][:, c, :],
                                                    start=False, stop=False, skip_group_check=True)
                        last.then_inc(s_hist_used[b], 1)
                nc.tensor.matmul(ps_hist[:, 0:NT], zero_bf[:, 0:P], zero_bf[:, 0:NT], start=False, stop=True,
                                 skip_group_check=True).then_inc(s_hist_done, 1)

            def single(dst, lhsT, rhs):
                asked[0] += 1
                pe.wait_ge(s_pe_ask, asked[0])
                nc.tensor.matmul(dst, lhsT, rhs, start=True, stop=True).then_inc(s_pe_done, 1)

            def linear(fi, fo, w):
                base = NG * lin[0]
                lin[0] += 1
                with pe.Fori(0, NG) as g:
                    pe.wait_ge(s_lin_in, g + (base + 1))
                    pe.nop(nofuse=True)
                    for u in range(G):
                        last = nc.tensor.transpose(ps_T[0:fi, u * P:(u + 1) * P], stage[:, u, 0:fi], ident[:, :])
                    last.then_inc(s_lin_T, 1)
                    pe.wait_ge(s_lin_S, g + (base + 1))
                    for u in range(G):
                        last = nc.tensor.matmul(ps_Y[:, u * P:u * P + fo], staged_T[0:fi, u * P:(u + 1) * P], w,
                                                start=True, stop=True)
                    last.then_inc(s_lin_out, 1)

            def extras(w):
                base = NG * xtr[0]
                xtr[0] += 1
                with pe.Fori(0, NG) as g:
                    pe.wait_ge(s_x_in, g + (base + 1))
                    nc.tensor.matmul(ps_misc[:, 0:G * w], onehot_p[:, :], stage[:, :, :].rearrange("p g f -> p (g f)")[:, 0:G * w],
                                     start=True, stop=True).then_inc(s_x_out, 1)

            def sheaf_pass():
                pairs = pair.rearrange("p c f -> p (c f)")
                with pe.Fori(0, NCH) as c:
                    pe.wait_ge(s_pair, c + 1)
                    for g in range(GROUPS4):
                        n = 32 * cols_of(g)
                        last = nc.tensor.transpose(ps_T[0:n, g * P:(g + 1) * P], pairs[:, 128 * g:128 * g + n], ident[:, :])
                    last.then_inc(s_pair_T, 1)
                    pe.wait_ge(s_pair_S, c + 1)

                    def second_layer(g):
                        pe.wait_ge(s_hid_relu, c * GROUPS4 + (g + 1))
                        for u in range(cols_of(g)):
                            col = 4 * g + u
                            last = nc.tensor.matmul(ps_Y[:, 32 * col:32 * col + 32], hidden[g % 2][:, u * P:(u + 1) * P],
                                                    w_refl2[:, :], start=True, stop=True)
                        last.then_inc(s_refl, 1)

                    for g in range(GROUPS4):
                        kk = 32 * cols_of(g)
                        for u in range(cols_of(g)):
                            last = nc.tensor.matmul(ps_hist[:, 512 * (g % 2) + u * P:512 * (g % 2) + (u + 1) * P],
                                                    w_refl1[0:kk, u, :], pair_T[0:kk, g * P:(g + 1) * P],
                                                    start=True, stop=True)
                        last.then_inc(s_hid, 1)
                        if g >= 1:
                            second_layer(g - 1)
                    second_layer(GROUPS4 - 1)
                    pe.wait_ge(s_src_row, c + 1)

                    def src_wide(g):
                        for u in range(cols_of(g)):
                            last = nc.tensor.matmul(ps_misc[:, u * P:(u + 1) * P],
                                                    src_f[:, 4 * g + u:4 * g + u + 1].to_broadcast([P, P]), ident[:, :],
                                                    start=True, stop=True)
                        last.then_inc(s_src_wide, 1)

                    src_wide(0)
                    for g in range(GROUPS4):
                        pe.wait_ge(s_equal, c * GROUPS4 + (g + 1))
                        if g + 1 < GROUPS4:
                            src_wide(g + 1)
                        if g == 0:
                            pe.wait_ge(s_msg, c + 1)
                        for u in range(cols_of(g)):
                            col = 4 * g + u
                            last = nc.tensor.matmul(ps_misc[:, 512 + 16 * col:512 + 16 * col + 16],
                                                    equal[g % 2][:, u * P:(u + 1) * P], once[:, 32 * col:32 * col + 16],
                                                    start=True, stop=True)
                        last.then_inc(s_summed, 1)

            for b in range(NB):
                pe.sem_inc(s_hist_used[b], 1)
            count(0)
            single(ps_misc[:, 0:NT], upto[:, :], cnt[:, :])
            single(ps_misc[:, P:P + NT], ones[:, :], cnt[:, :])
            single(ps_misc[:, 512:512 + P], wide[:, :], ident[:, :])
            count(1)
            extras(RUN_W[GCN1])
            linear(16, 32, w_gcn1[:, :])
            linear(32, 16, w_gcn2[:, :])
            extras(RUN_W[GCN2])
            linear(16, 6, w_att1[:, :])
            for h in range(3):
                single(ps_misc[:, 512:512 + P], wide[:, :], ident[:, :])
            extras(RUN_W[GAT1] + 1)
            linear(48, 96, w_heads[:, :])
            linear(96, 34, w_gat2[:, :])
            single(ps_misc[:, 512:512 + P], wide[:, :], ident[:, :])
            extras(RUN_W[GAT2] + 1)
            linear(32, 16, w_fin[:, :])
            sheaf_pass()
            extras(RUN_W[SHEAF])
            linear(16, 128, w_rel1[:, 0:128])
            linear(16, 128, w_rel1[:, 128:256])
            linear(16, 32, w_root1[:, :])
            extras(RUN_W[REL1])
            linear(32, 128, w_rel2[:, :])
            linear(32, 16, w_root2[:, :])
            extras(RUN_W[REL2])

        @block.vector
        def _(v):
            V = nc.vector
            step = [0]

            def then(ins):
                step[0] += 1
                ins.then_inc(s_order, 1)
                v.wait_ge(s_order, step[0])
                return ins

            def fresh():
                v.sem_clear(s_order)
                step[0] = 0

            def tt(o, a, b, op):
                return V.tensor_tensor(o, a, b, op)

            def ts(o, a, s1, s2, op0, op1=None):
                if op1 is None:
                    return V.tensor_scalar(o, a, s1, None, op0)
                return V.tensor_scalar(o, a, s1, s2, op0, op1)

            def bc_last(ap, n):
                return ap.unsqueeze(len(ap.shape)).to_broadcast(list(ap.shape) + [n])

            def bc_mid(ap, n):
                return ap.unsqueeze(1).to_broadcast([ap.shape[0], n] + list(ap.shape[1:]))

            asks = {"pe": 0, "act": 0}

            def ask_act():
                asks["act"] += 1
                v.sem_inc(s_act_ask, 1)
                v.wait_ge(s_act_done, asks["act"])

            def ask_pe(n=1):
                asks["pe"] += n
                v.sem_inc(s_pe_ask, n)
                v.wait_ge(s_pe_done, asks["pe"])

            def inverse_sqrt(dst):
                ask_act()
                then(V.reciprocal(dst, small[:, 1, :]))

            def layer_norm():
                sq = nodes(scratch, 16)
                then(V.tensor_reduce(small[:, 2, :], x[:, :, :], AX.X, ALU.add))
                then(ts(small[:, 2, :], small[:, 2, :], 1.0 / 16, None, ALU.mult))
                then(tt(hn[:, :, :], x[:, :, :], bc_last(small[:, 2, :], 16), ALU.subtract))
                then(tt(sq, hn[:, :, :], hn[:, :, :], ALU.mult))
                then(V.tensor_reduce(small[:, 2, :], sq, AX.X, ALU.add))
                then(ts(small[:, 0, :], small[:, 2, :], 1.0 / 16, EPS, ALU.mult, ALU.add))
                inverse_sqrt(small[:, 3, :])
                then(tt(hn[:, :, :], hn[:, :, :], bc_last(small[:, 3, :], 16), ALU.mult))
                then(ts(hn[:, :, :], hn[:, :, :], 0.0, None, ALU.max))

            lin = [0]
            xtr = [0]

            def linear(dst, src, fi, fo):
                base = NG * lin[0]
                lin[0] += 1
                with v.Fori(0, NG) as g:
                    fresh()
                    V.tensor_copy(stage[:, :, 0:fi], src[:, bass.ds(g * G, G), :]).then_inc(s_lin_in, 1)
                    v.wait_ge(s_lin_out, g + (base + 1))
                    v.nop(nofuse=True)
                    then(V.tensor_copy(dst[:, bass.ds(g * G, G), :],
                                       ps_Y[:, 0:G * P].rearrange("p (g f) -> p g f", f=P)[:, :, 0:fo]))

            def extras(w):
                base = NG * xtr[0]
                xtr[0] += 1
                dst = nodes(scratch, w)
                op = stage[:, :, :].rearrange("p g f -> p (g f)")[:, 0:G * w].rearrange("p (g f) -> p g f", f=w)
                with v.Fori(0, NG) as g:
                    fresh()
                    tt(op, bc_last(onehot_t[:, bass.ds(g * G, G)], w), bc_mid(tail[:, 0:w], G), ALU.mult).then_inc(s_x_in, 1)
                    v.wait_ge(s_x_out, g + (base + 1))
                    v.nop(nofuse=True)
                    then(V.tensor_copy(dst[:, bass.ds(g * G, G), :], ps_misc[:, 0:G * w].rearrange("p (g f) -> p g f", f=w)))
                return dst

            def pass_done(k):
                w = RUN_W[k]
                v.wait_ge(s_run[NB - 1], NIT * (k + 1))
                for b in range(NB):
                    v.wait_ge(s_kept[b], 16 * (NIT * (k + 1) + 1))
                then(V.tensor_copy(tail[:, 0:w], run_view(NB - 1, w)[:, C - 1, :]))

            def ends_in(k):
                v.wait_ge(s_ends, N_ENDS * (k + 1))
                return nodes(ends, RUN_W[k])

            def summed(k):
                w = RUN_W[k]
                pass_done(k)
                more = extras(w)
                total = ends_in(k)
                then(tt(total, total, bc_last(has[:, :], w), ALU.mult))
                then(tt(total, total, more, ALU.add))
                return total

            def selu(z, f):
                e = nodes(scratch, f)
                then(ts(e, z, 0.0, None, ALU.min))
                ask_act()
                then(ts(e, e, SELU_S * SELU_A, -SELU_S * SELU_A, ALU.mult, ALU.add))
                then(ts(z, z, 0.0, SELU_S, ALU.max, ALU.mult))
                then(tt(z, z, e, ALU.add))

            def gat_nodes(k):
                heads, d, w = HEADS[k], HEAD_D[k], RUN_W[k]
                o, m0 = heads * d, heads * d + heads
                pass_done(k)
                for h in range(heads):
                    then(V.tensor_copy(wide[:, :], tail[:, m0 + h:m0 + h + 1].to_broadcast([P, P])))
                    ask_pe()
                    then(tt(wide[:, :], ps_misc[:, 512:512 + P], not_same_node[:, :], ALU.add))
                    then(V.tensor_reduce(tail_m[:, h:h + 1], wide[:, :], AX.X, ALU.max))
                then(tt(tail_m[:, 3:3 + heads], tail[:, m0:m0 + heads], tail_m[:, 0:heads], ALU.subtract))
                then(ts(tail_m[:, 3:3 + heads], tail_m[:, 3:3 + heads], 0.0, None, ALU.min))
                ask_act()
                for h in range(heads):
                    ts(tail[:, h * d:(h + 1) * d], tail[:, h * d:(h + 1) * d], tail_m[:, 3 + h:4 + h], None, ALU.mult)
                then(tt(tail[:, o:o + heads], tail[:, o:o + heads], tail_m[:, 3:3 + heads], ALU.mult))
                ts(tail[:, m0:m0 + heads], tail_m[:, 0:heads], rep[:, 0:1], None, ALU.mult)
                then(V.tensor_copy(tail[:, w:w + 1], rep[:, 0:1]))
                more = extras(w + 1)
                end = ends_in(k)
                merge = work[:, 9408:9408 + 3 * heads * NT].rearrange("p (s t h) -> p s t h", s=3, h=heads)
                top = work[:, 9408 + 9 * NT:9408 + (9 + heads) * NT].rearrange("p (t h) -> p t h", h=heads)
                tot = work[:, 9408 + 12 * NT:9408 + (12 + heads) * NT].rearrange("p (t h) -> p t h", h=heads)
                att = nodes(node_rows, ROW_F[k])
                own, tails, loop = merge[:, 0], merge[:, 1], merge[:, 2]
                ts(small[:, 0, :], has[:, :], -1.0, BIG, ALU.add, ALU.mult)
                then(ts(small[:, 1, :], more[:, :, w], -1.0, BIG, ALU.add, ALU.mult))
                tt(own, end[:, :, m0:m0 + heads], bc_last(has[:, :], heads), ALU.mult)
                tt(tails, more[:, :, m0:m0 + heads], bc_last(small[:, 1, :], heads), ALU.add)
                then(tt(loop, att[:, :, d:d + heads], att[:, :, d + heads:d + 2 * heads], ALU.add))
                then(tt(own, own, bc_last(small[:, 0, :], heads), ALU.add))
                then(V.scalar_tensor_tensor(tot, loop, SLOPE, loop, ALU.mult, ALU.max))
                then(V.tensor_copy(loop, tot))
                then(tt(top, own, tails, ALU.max))
                then(tt(top, top, loop, ALU.max))
                for part in (own, tails, loop):
                    last = tt(part, part, top, ALU.subtract)
                then(last)
                ask_act()
                then(tt(tot, end[:, :, o:o + heads], own, ALU.mult))
                then(tt(top, more[:, :, o:o + heads], tails, ALU.mult))
                then(tt(tot, tot, top, ALU.add))
                then(tt(tot, tot, loop, ALU.add))
                then(ts(tot, tot, 1e-16, None, ALU.add))
                then(V.reciprocal(top, tot))
                self_rows = hn[:, :, :] if k == GAT1 else att[:, :, 0:d]
                part = work[:, 0:NT * d].rearrange("p (t f) -> p t f", f=d)
                for h in range(heads):
                    of = end[:, :, h * d:(h + 1) * d]
                    then(tt(of, of, bc_last(own[:, :, h], d), ALU.mult))
                    then(tt(part, more[:, :, h * d:(h + 1) * d], bc_last(tails[:, :, h], d), ALU.mult))
                    then(tt(of, of, part, ALU.add))
                    then(tt(part, self_rows, bc_last(loop[:, :, h], d), ALU.mult))
                    then(tt(of, of, part, ALU.add))
                    then(tt(of, of, bc_last(top[:, :, h], d), ALU.mult))
                return end[:, :, 0:o]

            def hand_indices(k, b, c):
                at_c = bass.ds(c * C, C)
                if k < REL1:
                    V.tensor_copy(idx_chunk[b][:, :], row_of_src[:, at_c]).then_inc(s_idx[b], 1)
                else:
                    V.scalar_tensor_tensor(idx_chunk[b][:, :], row_of_src[:, at_c], float(REL), etype[:, at_c],
                                           ALU.mult, ALU.add).then_inc(s_idx[b], 1)

            def scans(k, b, lanes, carry_on, values, start=0):
                cur, prev = run_view(b, RUN_W[k]), run_view((b - 1) % NB, RUN_W[k])
                for f in range(lanes):
                    last = V.tensor_tensor_scan(cur[:, :, start + f], carry_on, values[:, :, f],
                                                prev[:, C - 1, start + f:start + f + 1], ALU.mult, ALU.add)
                return last

            def count_step(c, kh, turn):
                for b in range(NB):
                    v.wait_ge(s_hist_used[b], turn + (NCH * kh + 1))
                    cc = bass.ds(c * C + b * HC, HC)
                    tt(hist_lo[b], bc_last(lo_all[:, cc], P), bc_mid(iota_bf[:, :], HC), ALU.is_equal)
                    tt(hist_hi[b], bc_last(hi_all[:, cc], NT), bc_mid(iota_bf[:, 0:NT], HC), ALU.is_equal).then_inc(s_hist_ready[b], 1)

            def spread_values(k, b, i, into=None):
                n = SPREAD[k]
                sv = spread_view(b, n)
                v.wait_ge(s_spread_in[b], (i + (NIT * SPREAD_NO[k] + 1)) * 16)
                then(tt(sv, sv, bc_last(start_c[:, :], n), ALU.mult))
                for f in range(n):
                    dst = sv[:, :, f] if into is None else into(f)
                    last = V.tensor_tensor_scan(dst, same_c[:, :], sv[:, :, f], carry[:, f:f + 1], ALU.mult, ALU.add)
                then(last)
                if into is None:
                    then(V.tensor_copy(carry[:, 0:n], sv[:, C - 1, :]))
                return sv

            def edge_chunk(k, i, b):
                c = i * NB + b
                at_c = bass.ds(c * C, C)
                w, f_in = RUN_W[k], ROW_F[k]
                rows, run, prev = rows_view(b, f_in), run_view(b, w), run_view((b - 1) % NB, w)
                V.tensor_copy(same_c[:, :], same[:, at_c])
                then(ts(start_c[:, :], same[:, at_c], -1.0, 1.0, ALU.mult, ALU.add))
                if k == GCN1:
                    then(tt(type_onehot, bc_last(etype[:, at_c], REL), bc_mid(iota_bf[:, 0:REL], C), ALU.is_equal))
                    count_step(c, 1, c)
                if k == REL1:
                    spread = spread_values(k, b, i)
                    then(tt(rel_onehot, bc_last(etype[:, at_c], REL), bc_mid(iota_bf[:, 0:REL], C), ALU.is_equal))
                    then(tt(rel_onehot, rel_onehot, spread, ALU.mult))
                    then(V.tensor_reduce(rel_w, rel_onehot, AX.X, ALU.add))
                    V.tensor_copy(edge_weight[:, at_c], rel_w)
                if k == REL2:
                    then(V.tensor_copy(rel_w, edge_weight[:, at_c]))
                if k in HEADS:
                    spread = spread_values(k, b, i)
                    then(ts(neg_c[:, :], same_c[:, :], -1.0, BIG, ALU.add, ALU.mult))
                if k < LATER:
                    v.wait_ge(s_got_early[b], (i + (NIT * k + 1)) * (16 * C))
                else:
                    v.wait_ge(s_got_later[b], (i + (NIT * (k - LATER) + 1)) * (16 * C))
                v.wait_ge(s_kept[b], (i + (NIT * k + 1)) * 16)
                if k == GCN1:
                    scans(k, b, 16, same_c[:, :], rows)
                    last = scans(k, b, REL, same_c[:, :], type_onehot, 16)
                elif k == GCN2:
                    last = scans(k, b, 16, same_c[:, :], rows)
                elif k in (REL1, REL2):
                    then(tt(rows, rows, bc_last(rel_w, f_in), ALU.mult))
                    last = scans(k, b, w, same_c[:, :], rows)
                elif k in HEADS:
                    heads, d = HEADS[k], HEAD_D[k]
                    o, m0 = heads * d, heads * d + heads
                    lanes = lambda t, n: t[:, 0:C * n].rearrange("p (c h) -> p c h", h=n)
                    raw, score, ein, eout, rat = lanes(score0, heads), lanes(score1, heads), lanes(exp_in, 2 * heads), \
                        lanes(exp_out, 2 * heads), lanes(ratio, heads)
                    msg = lanes(gat_msg, o)
                    then(tt(raw, rows[:, :, d:d + heads], spread, ALU.add))
                    then(V.scalar_tensor_tensor(score, raw, SLOPE, raw, ALU.mult, ALU.max))
                    for h in range(heads):
                        last = V.tensor_tensor_scan(run[:, :, m0 + h], neg_c[:, :], score[:, :, h],
                                                    prev[:, C - 1, m0 + h:m0 + h + 1], ALU.add, ALU.max)
                    then(last)
                    mx = run[:, :, m0:m0 + heads]
                    tt(ein[:, 1:C, 0:heads], mx[:, 0:C - 1, :], mx[:, 1:C, :], ALU.subtract)
                    tt(ein[:, 0, 0:heads], prev[:, C - 1, m0:m0 + heads], mx[:, 0, :], ALU.subtract)
                    then(tt(ein[:, :, heads:2 * heads], score, mx, ALU.subtract))
                    ts(ein, ein, 0.0, None, ALU.min).then_inc(s_gat_in, 1)
                    v.wait_ge(s_gat_exp, c + (NCH * (k - GAT1) + 1))
                    tt(rat, eout[:, :, 0:heads], bc_last(same_c[:, :], heads), ALU.mult)
                    for h in range(heads):
                        last = tt(msg[:, :, h * d:(h + 1) * d], rows[:, :, 0:d], bc_last(eout[:, :, heads + h], d), ALU.mult)
                    then(last)
                    for h in range(heads):
                        scans(k, b, d, rat[:, :, h], msg[:, :, h * d:(h + 1) * d], h * d)
                        last = scans(k, b, 1, rat[:, :, h], eout[:, :, heads + h:heads + h + 1], o + h)
                else:
                    last = sheaf_chunk(i, b, c, rows)
                then(last)
                v.sem_inc(s_run[b], 1)
                hand_indices(k, b, c + NB)

            def sheaf_chunk(i, b, c, rows):
                as32 = lambda t: t.rearrange("p (c f) -> p c f", f=32)
                as2 = lambda t: t.rearrange("p (c s f) -> p (c s) f", s=2, f=16)
                vec, pr, y = as32(refl), as32(prod), as32(once)
                flat = pair.rearrange("p c f -> p (c f)")
                V.tensor_copy(pair[:, :, 0:16], rows[:, :, 0:16])
                then(V.tensor_copy(src_f, row_of_src[:, bass.ds(c * C, C)]))
                v.sem_inc(s_src_row, 1)
                sv = spread_values(SHEAF, b, i, lambda f: pair[:, :, 16 + f] if f < 16 else fill_dis)
                V.tensor_copy(carry[:, 0:16], pair[:, C - 1, 16:32])
                then(V.tensor_copy(carry[:, 16:17], fill_dis[:, C - 1:C]))
                v.sem_inc(s_pair, 1)

                def equality(g):
                    n = cols_of(g)
                    v.wait_ge(s_src_wide, c * GROUPS4 + (g + 1))
                    if g >= 2:
                        v.wait_ge(s_summed, c * GROUPS4 + (g - 1))
                    eq = equal[g % 2][:, 0:n * P].rearrange("p (u q) -> p u q", q=P)
                    before = earlier[:, 0:n * P].rearrange("p (u q) -> p u q", q=P)
                    then(tt(eq, ps_misc[:, 0:n * P].rearrange("p (u q) -> p u q", q=P),
                            bc_last(src_f[:, 4 * g:4 * g + n], P), ALU.is_equal))
                    v.sem_inc(s_equal, 1)
                    then(tt(before, eq, bc_mid(below[:, :], n), ALU.mult))
                    then(V.tensor_reduce(rank[:, 4 * g:4 * g + n], before, AX.X, ALU.add))

                v.wait_ge(s_refl, (c + 1) * GROUPS4)
                then(tt(vec, ps_Y[:, 0:C * 32].rearrange("p (c f) -> p c f", f=32), bc_mid(b_refl2, C), ALU.add))
                tt(pr, vec, vec, ALU.mult)
                then(tt(y, vec, pair, ALU.mult))
                V.tensor_reduce(inv2, as2(prod), AX.X, ALU.add)
                then(V.tensor_reduce(dots, as2(once), AX.X, ALU.add))
                then(ts(inv2, inv2, 1e-24, None, ALU.max))
                then(V.reciprocal(inv2, inv2))
                then(V.scalar_tensor_tensor(dots, dots, 2.0, inv2, ALU.mult, ALU.mult))
                then(tt(as2(prod), as2(refl), bc_last(dots, 16), ALU.mult))
                tt(y[:, :, 0:16], pair[:, :, 16:32], pr[:, :, 16:32], ALU.subtract)
                then(tt(y[:, :, 16:32], pair[:, :, 0:16], pr[:, :, 0:16], ALU.subtract))
                then(tt(pr, vec, y, ALU.mult))
                then(V.tensor_reduce(dots, as2(prod), AX.X, ALU.add))
                then(V.scalar_tensor_tensor(dots, dots, 2.0, inv2, ALU.mult, ALU.mult))
                then(tt(as2(prod), as2(refl), bc_last(dots, 16), ALU.mult))
                then(tt(y, y, pr, ALU.subtract))
                tt(y[:, :, 0:16], y[:, :, 0:16], bc_last(fill_dis, 16), ALU.mult)
                then(tt(y[:, :, 16:32], y[:, :, 16:32], bc_last(rows[:, :, 16], 16), ALU.mult))
                v.sem_inc(s_msg, 1)
                for g in range(GROUPS4):
                    equality(g)
                then(ts(rank, rank, 0.5, None, ALU.is_lt))
                then(ts(src_f, src_f, spare_node[:, 0:1], None, ALU.subtract))
                then(tt(src_f, src_f, rank, ALU.mult))
                ts(add_idx[b][:, :], src_f, spare_node[:, 0:1], None, ALU.add)
                v.wait_ge(s_summed, (c + 1) * GROUPS4)
                V.tensor_copy(add_rows[b][:, :, :], ps_misc[:, 512:512 + C * 16].rearrange("p (c f) -> p c f", f=16)).then_inc(s_add_ready[b], 1)
                return scans(SHEAF, b, 16, same_c[:, :], y[:, :, 16:32])

            def edge_pass(k):
                w = RUN_W[k]
                v.wait_ge(s_rows_stored, 16 * TABLES_BEFORE[k])
                fresh()
                zero_tail = run_view(NB - 1, w)[:, C - 1, :]
                then(V.memset(zero_tail, 0.0))
                if k in HEADS:
                    then(V.memset(zero_tail[:, w - HEADS[k]:w], -BIG))
                for b in range(NB):
                    hand_indices(k, b, b)
                if k in SPREAD:
                    v.wait_ge(s_first, 16 * (SPREAD_NO[k] + 1))
                    then(V.tensor_copy(carry[:, 0:SPREAD[k]], first_row[:, SPREAD_AT[k]:SPREAD_AT[k] + SPREAD[k]]))
                with v.Fori(0, NIT) as i:
                    fresh()
                    for b in range(NB):
                        edge_chunk(k, i, b)

            V.memset(w_heads[:, :], 0.0)
            V.memset(w_refl2[:, :], 0.0)
            V.memset(w_refl1[:, :, :], 0.0)
            V.memset(x[:, NT - 1, :], 0.0)
            V.memset(scratch[:, 8000:8192], 0.0)
            then(V.memset(ends[:, 0:(EDGES + P) // P], 0.0))
            v.sem_inc(s_zero_src, 1)
            V.memset(ones[:, :], 1.0)
            V.memset(same_c[:, :], 0.0)
            V.memset(row_of_src[:, COLS:COLS + NB * C], 0)
            V.memset(etype[:, COLS:COLS + NB * C], 0.0)
            v.wait_ge(s_iota, 2)
            V.tensor_copy(iota_bf[:, :], iota_row[:, :])
            ts(ident[:, :], iota_row[:, :], iota_p[:, 0:1], None, ALU.is_equal)
            ts(upto[:, :], iota_row[:, :], iota_p[:, 0:1], None, ALU.is_ge)
            ts(below[:, :], iota_row[:, :], iota_p[:, 0:1], None, ALU.is_lt)
            ts(spare_edge[:, :], iota_p[:, :], float(EDGES), None, ALU.add)
            then(ts(spare_node[:, :], iota_p[:, :], float(ROWS), None, ALU.add))
            v.wait_ge(s_loads, 16 * N_LOADS)
            raw = work[:, :].bitcast(I32)
            dst_raw, src_raw, type_raw = raw[:, 0:COLS], raw[:, COLS:2 * COLS], raw[:, 2 * COLS:3 * COLS]
            low_tmp = raw[:, 3 * COLS:4 * COLS]
            split = lambda o, a, op, n: V.tensor_single_scalar(o, a, n, op)
            V.tensor_copy(etype[:, 0:COLS], type_raw)
            V.memset(same[:, 0:1], 1.0)
            tt(same[:, 1:COLS], dst_raw[:, 1:COLS], dst_raw[:, 0:COLS - 1], ALU.is_equal)

            def low_high(ids):
                then(split(low_tmp, ids, ALU.bitwise_and, P - 1))
                then(V.tensor_copy(lo_all, low_tmp))
                then(split(low_tmp, ids, ALU.logical_shift_right, 7))
                then(V.tensor_copy(hi_all, low_tmp))

            low_high(dst_raw)
            v.sem_inc(s_hist_zero, 1)
            fresh()
            with v.Fori(0, NCH) as i:
                count_step(i, 0, i)
            v.wait_ge(s_hist_done, 1)
            then(V.tensor_copy(cnt[:, :], ps_hist[:, 0:NT]))
            low_high(src_raw)
            then(V.scalar_tensor_tensor(row_of_src[:, 0:COLS], lo_all, float(NT), hi_all, ALU.mult, ALU.add))
            v.sem_inc(s_hist_zero, 1)
            ask_pe(2)
            then(V.tensor_copy(small[:, 1, :], ps_misc[:, P:P + NT]))
            then(V.tensor_tensor_scan(small[:, 2, :], ones[:, 0:NT], small[:, 1, :], 0.0, ALU.mult, ALU.add))
            then(tt(small[:, 2, :], small[:, 2, :], small[:, 1, :], ALU.subtract))
            then(tt(small[:, 3, :], ps_misc[:, 0:NT], small[:, 2, :], ALU.add))
            then(ts(small[:, 1, :], small[:, 3, :], -1.0, 0.0, ALU.add, ALU.max))
            V.tensor_copy(end_idx[:, :], small[:, 1, :])
            then(ts(has[:, :], cnt[:, :], 0.5, None, ALU.is_gt))
            then(tt(small[:, 3, :], small[:, 3, :], cnt[:, :], ALU.subtract))
            then(ts(small[:, 3, :], small[:, 3, :], spare_edge[:, 0:1], None, ALU.subtract))
            then(tt(small[:, 3, :], small[:, 3, :], has[:, :], ALU.mult))
            then(ts(start_idx[:, :], small[:, 3, :], spare_edge[:, 0:1], None, ALU.add))
            lo_hi_i = raw[:, 0:4]
            then(split(lo_hi_i[:, 0:2], bounds[:, 0:2], ALU.bitwise_and, P - 1))
            then(split(lo_hi_i[:, 2:4], bounds[:, 0:2], ALU.logical_shift_right, 7))
            then(V.tensor_copy(bnd[:, 0:4], lo_hi_i))
            then(V.tensor_copy(bnd[:, 4:6], bounds[:, 1:3]))
            then(V.scalar_tensor_tensor(first_idx[:, :], bnd[:, 0:1], float(NT), bnd[:, 2:3], ALU.mult, ALU.add))
            then(tt(bnd[:, 6:7], bnd[:, 4:5], bnd[:, 5:6], ALU.is_equal))
            then(ts(bnd[:, 7:8], iota_p[:, :], P - 1.5, None, ALU.is_lt))
            then(tt(bnd[:, 6:7], bnd[:, 6:7], bnd[:, 7:8], ALU.mult))
            then(ts(onehot_p[:, :], iota_row[:, :], bnd[:, 1:2], bnd[:, 6:7], ALU.is_equal, ALU.mult))
            then(ts(onehot_t[:, :], iota_row[:, 0:NT], bnd[:, 3:4], None, ALU.is_equal))
            then(ts(bnd[:, 8:9], bnd[:, 4:5], 1.0, None, ALU.add))
            then(tt(bnd[:, 8:9], bnd[:, 8:9], bnd[:, 6:7], ALU.mult))
            then(V.tensor_copy(wide[:, :], bnd[:, 8:9].to_broadcast([P, P])))
            ask_pe()
            then(ts(bnd[:, 9:10], bnd[:, 4:5], 1.0, None, ALU.add))
            then(ts(wide[:, :], ps_misc[:, 512:512 + P], bnd[:, 9:10], None, ALU.is_equal))
            ts(not_same_node[:, :], wide[:, :], -1.0, BIG, ALU.add, ALU.mult)
            then(tt(wide[:, :], wide[:, :], below[:, :], ALU.mult))
            then(V.tensor_reduce(bnd[:, 10:11], wide[:, :], AX.X, ALU.add))
            then(ts(rep[:, :], bnd[:, 10:11], 0.5, bnd[:, 6:7], ALU.is_lt, ALU.mult))
            for s in range(2):
                then(tt(a_gat1w[:, s, :], w_gat1[:, :], a_gat1[:, s, :], ALU.mult))
                then(V.tensor_reduce(w_att1[:, 3 * s:3 * s + 3], a_gat1w[:, s, :].rearrange("p (h c) -> p h c", c=32), AX.X, ALU.add))
                then(tt(a_gat2[:, s, :], w_gat2[:, 0:32], a_gat2[:, s, :], ALU.mult))
                then(V.tensor_reduce(w_gat2[:, 32 + s:33 + s], a_gat2[:, s, :], AX.X, ALU.add))

            layer_norm()
            then(ts(small[:, 0, :], cnt[:, :], 1.0, None, ALU.add))
            inverse_sqrt(dinv[:, :])
            rows16 = nodes(node_rows, 16)
            then(tt(rows16, hn[:, :, :], bc_last(dinv[:, :], 16), ALU.mult))
            v.sem_inc(s_rows_ready, 1)
            edge_pass(GCN1)
            total = summed(GCN1)
            then(ts(inv_count[:, :, :], total[:, :, 16:24], 1.0, None, ALU.max))
            then(V.reciprocal(inv_count[:, :, :], inv_count[:, :, :]))
            v.wait_ge(s_hist_done, 2)
            then(tt(cnt[:, :], cnt[:, :], ps_hist[:, 0:NT], ALU.add))
            agg = total[:, :, 0:16]
            then(tt(agg, agg, rows16, ALU.add))
            then(tt(agg, agg, bc_last(dinv[:, :], 16), ALU.mult))
            hid = nodes(work, 32)
            linear(hid, agg, 16, 32)
            then(tt(hid, hid, bc_mid(b_gcn1, NT), ALU.add))
            then(ts(hid, hid, 0.0, None, ALU.max))
            linear(rows16, hid, 32, 16)
            then(tt(rows16, rows16, bc_last(dinv[:, :], 16), ALU.mult))
            v.sem_inc(s_rows_ready, 1)
            edge_pass(GCN2)
            total = summed(GCN2)
            then(tt(total, total, rows16, ALU.add))
            then(tt(total, total, bc_last(dinv[:, :], 16), ALU.mult))
            then(tt(total, total, bc_mid(b_gcn2, NT), ALU.add))
            then(tt(x[:, :, :], x[:, :, :], total, ALU.add))

            layer_norm()
            rows_gat1 = nodes(node_rows, 22)
            then(V.tensor_copy(rows_gat1[:, :, 0:16], hn[:, :, :]))
            linear(rows_gat1[:, :, 16:22], hn[:, :, :], 16, 6)
            v.sem_inc(s_rows_ready, 1)
            edge_pass(GAT1)
            agg = gat_nodes(GAT1)
            hid = nodes(work, 96)
            v.wait_ge(s_blk, 16 * 21)
            linear(hid, agg, 48, 96)
            then(tt(hid, hid, bc_mid(b_gat1, NT), ALU.add))
            for half in range(2):
                selu(hid[:, :, 48 * half:48 * half + 48], 48)
            rows_gat2 = nodes(node_rows, 34)
            linear(rows_gat2, hid, 96, 34)
            v.sem_inc(s_rows_ready, 1)
            edge_pass(GAT2)
            agg = gat_nodes(GAT2)
            then(tt(agg, agg, bc_mid(b_gat2, NT), ALU.add))
            selu(agg, 32)
            fin = nodes(work, 16)
            linear(fin, agg, 32, 16)
            then(tt(fin, fin, bc_mid(b_fin, NT), ALU.add))
            then(tt(x[:, :, :], x[:, :, :], fin, ALU.add))

            layer_norm()
            then(ts(small[:, 0, :], cnt[:, :], 1e-5, None, ALU.max))
            inverse_sqrt(dis[:, :])
            rows_sheaf = nodes(node_rows, 17)
            V.tensor_copy(rows_sheaf[:, :, 0:16], hn[:, :, :])
            then(V.tensor_copy(rows_sheaf[:, :, 16], dis[:, :]))
            v.sem_inc(s_rows_ready, 1)
            edge_pass(SHEAF)
            total = summed(SHEAF)
            v.sem_inc(s_acc_go, 1)
            part = nodes(scratch, 16)
            for n in range(C // ACC_ROUND):
                v.wait_ge(s_acc_in, 16 * ACC_ROUND * (n + 1))
                then(V.tensor_reduce(part, work[:, 0:ACC_ROUND * NT * 16].rearrange("p (m t f) -> p t f m", m=ACC_ROUND, f=16), AX.X, ALU.add))
                then(tt(total, total, part, ALU.add))
                v.sem_inc(s_acc_used, 1)
            then(tt(total, total, bc_last(dis[:, :], 16), ALU.mult))
            then(tt(total, total, hn[:, :, :], ALU.add))
            then(ts(total, total, 0.0, None, ALU.max))
            then(tt(x[:, :, :], x[:, :, :], total, ALU.add))

            layer_norm()
            v.sem_inc(s_rows_ready, 1)
            for half in range(2):
                if half:
                    v.wait_ge(s_rows_stored, 16 * (T_REL1A + 1))
                linear(nodes(work, P), hn[:, :, :], 16, P)
                v.sem_inc(s_rows_ready, 1)
            root1 = nodes(node_rows, 32)
            linear(root1, hn[:, :, :], 16, 32)
            then(tt(root1, root1, bc_mid(b_rel1, NT), ALU.add))
            edge_pass(REL1)
            total = summed(REL1)
            then(tt(total, total, root1, ALU.add))
            then(ts(total, total, 0.0, None, ALU.max))
            linear(nodes(work, P), total, 32, P)
            v.sem_inc(s_rows_ready, 1)
            root2 = nodes(node_rows, 16)
            linear(root2, total, 32, 16)
            then(tt(root2, root2, bc_mid(b_rel2, NT), ALU.add))
            edge_pass(REL2)
            total = summed(REL2)
            then(tt(total, total, root2, ALU.add))
            then(tt(x[:, :, :], x[:, :, :], total, ALU.add))
            v.sem_inc(s_final, 1)


_INS = ['x', 'src', 'dst', 'edge_type_8', 'L0_gnn_W1', 'L0_gnn_b1', 'L0_gnn_W2', 'L0_gnn_b2', 'L1_gnn_W1', 'L1_gnn_a_src1',
        'L1_gnn_a_dst1', 'L1_gnn_b1', 'L1_gnn_W2', 'L1_gnn_a_src2', 'L1_gnn_a_dst2', 'L1_gnn_b2', 'L1_gnn_Wf', 'L1_gnn_bf',
        'L2_gnn_W1', 'L2_gnn_b1', 'L2_gnn_W2', 'L2_gnn_b2', 'L3_gnn_W1', 'L3_gnn_root1', 'L3_gnn_b1', 'L3_gnn_W2',
        'L3_gnn_root2', 'L3_gnn_b2']


def kernel(**inputs):
    import numpy as _np
    import concourse.bacc as _bacc
    from concourse import mybir as _mybir
    from concourse.bass_utils import run_bass_kernel_spmd as _run

    nc = _bacc.Bacc("TRN2", target_bir_lowering=False, num_devices=1)
    arrays, args = {}, {}
    for name in _INS:
        a = _np.asarray(inputs[name])
        if name in ("L2_gnn_W1", "L2_gnn_W2"):
            a = a.T
        if name in ("L3_gnn_W1", "L3_gnn_W2"):
            a = a.transpose(1, 0, 2).reshape(a.shape[1], -1)
        a = _np.ascontiguousarray(a)
        arrays[f"in_{name}"] = a
        args[name] = nc.dram_tensor(f"in_{name}", a.shape, _mybir.dt.from_np(a.dtype), kind="ExternalInput").ap()
    out = nc.dram_tensor("out_x", (NODES, 16), _mybir.dt.float32, kind="ExternalOutput").ap()
    build_kernel(nc, args, out)
    r = _run(nc, [arrays], core_ids=[0])
    return r.results[0]["out_x"]
```

```python
import concourse.bass as bass
from concourse import mybir
from contextlib import ExitStack

F32 = mybir.dt.float32
BF16 = mybir.dt.bfloat16
I32 = mybir.dt.int32
ALU = mybir.AluOpType
ACT = mybir.ActivationFunctionType
AX = mybir.AxisListType

P = 128
NODES = 12500
EDGES = 400000
NT = (NODES + P - 1) // P
ROWS = NT * P
COLS = EDGES // P
C = 25
NB = 5
NCH = COLS // C
NIT = NCH // NB
HC = C // NB
BLK = 25
BLOCKS = EDGES // BLK
SAMPLES = COLS // BLK
G = 7
NG = NT // G
REL = 8
SCRATCH = 7040
BIG = 1e30
HALF = (C + 1) // 2
ACC_LOADS = [4, 4, 4, 1]
SLOPE = 0.2
EPS = 1e-5
SELU_A = 1.6732632423543772
SELU_S = 1.0507009873554805

GCN1, GCN2, GAT1, GAT2, SHEAF, REL1, REL2 = range(7)
ROW_F = [16, 16, 22, 34, 17, 32, 16]
RUN_W = [24, 16, 54, 34, 16, 32, 16]
SPREAD = {GAT1: 3, GAT2: 1, SHEAF: 17, REL1: 8}
SPREAD_AT = {GAT1: 19, GAT2: 33, SHEAF: 0, REL1: 0}
SPREAD_NO = {GAT1: 0, GAT2: 1, SHEAF: 2, REL1: 3}
SCATTERED = {GAT1: 2, GAT2: 3, SHEAF: 4, REL1: 1}
HEADS = {GAT1: 3, GAT2: 1}
HEAD_D = {GAT1: 16, GAT2: 32}
T_GCN1, T_INV, T_GCN2, T_GAT1, T_GAT2, T_SHEAF = range(6)
T_NODE = [T_GCN1, T_GCN2, T_GAT1, T_GAT2, T_SHEAF]
TABLES_BEFORE = [1, 3, 4, 5, 6]
REL_BEFORE = {REL1: 2, REL2: 3}
N_LOADS_DST = 5
N_LOADS = 28


def build_kernel(nc, A, out):
    ctx = ExitStack()
    with ctx:
        def sb(name, shape, dt=F32):
            return ctx.enter_context(nc.sbuf_tensor(name, shape, dt))

        def sem(name):
            return ctx.enter_context(nc.semaphore(name))

        def dram(name, shape, dt=F32):
            return nc.dram_tensor(name, shape, dt, kind="Internal").ap()

        tables = [dram(f"table{k}", (ROWS, f)) for k, f in enumerate([16, 16, 22, 34, 17])]
        inv_table = dram("inv_table", (ROWS, REL))
        rel1_table = dram("rel1_table", (ROWS * REL, 32))
        rel2_table = dram("rel2_table", (ROWS * REL, 16))
        gathered = tables + [rel1_table, rel2_table]
        running = [dram(f"running{k}", (EDGES, w)) for k, w in enumerate(RUN_W)]
        spread_rows = {k: dram(f"spread{k}", (EDGES + P, n)) for k, n in SPREAD.items()}
        acc_tables = [dram(f"acc{c}", (ROWS + P, 16)) for c in range(HALF)]

        row_of_src = sb("row_of_src", [P, COLS + NB * C], I32)
        etype = sb("etype", [P, COLS + NB * C], BF16)
        same = sb("same", [P, COLS], BF16)
        weight_lohi = sb("weight_lohi", [P, COLS])
        lohi = weight_lohi[:, :].bitcast(BF16)
        lo_all, hi_all = lohi[:, 0:COLS], lohi[:, COLS:2 * COLS]
        edge_weight = weight_lohi
        x = sb("x", [P, NT, 16])
        hn = sb("hn", [P, NT, 16])
        node_rows = sb("node_rows", [P, NT * 34])
        inv_count = sb("inv_count", [P, NT, REL])
        ends = sb("ends", [P, NT * 54])
        work = sb("work", [P, 13125])
        scratch = sb("scratch", [P, SCRATCH])
        cnt = sb("cnt", [P, NT])
        has = sb("has", [P, NT])
        dinv = sb("dinv", [P, NT])
        dis = sb("dis", [P, NT])
        end_idx = sb("end_idx", [P, NT], I32)
        start_idx = sb("start_idx", [P, NT], I32)
        block_idx = sb("block_idx", [P, NT], I32)
        small = sb("small", [P, 4, NT])
        ident = sb("ident", [P, P])
        ones = sb("ones", [P, P])
        upto = sb("upto", [P, P])
        below = sb("below", [P, P])
        iota_row = sb("iota_row", [P, P])
        iota_bf = sb("iota_bf", [P, P], BF16)
        iota_p = sb("iota_p", [P, 1])
        spare_edge = sb("spare_edge", [P, 1])
        spare_node = sb("spare_node", [P, 1])
        bounds = sb("bounds", [P, 3], I32)
        bnd = sb("bnd", [P, 12])
        first_idx = sb("first_idx", [P, 1], I32)
        first_row = sb("first_row", [P, 34])
        carry = sb("carry", [P, 17])
        onehot_p = sb("onehot_p", [P, P])
        onehot_t = sb("onehot_t", [P, NT])
        not_same_node = sb("not_same_node", [P, P])
        rep = sb("rep", [P, 1])
        tail = sb("tail", [P, 56])
        tail_m = sb("tail_m", [P, 9])
        wide = sb("wide", [P, P])
        idx_chunk = [sb(f"idx_chunk{b}", [P, C], I32) for b in range(NB)]
        add_idx = [sb(f"add_idx{b}", [P, C], I32) for b in range(NB)]
        add_rows = [sb(f"add_rows{b}", [P, C, 16]) for b in range(NB)]
        same_c = sb("same_c", [P, C])
        start_c = sb("start_c", [P, C])
        neg_c = sb("neg_c", [P, C])
        stages = [sb(f"stage{u}", [P, G, 96]) for u in range(2)]
        staged_T = [sb(f"staged_T{u}", [96, G * P]) for u in range(2)]
        bounds_lohi = sb("bounds_lohi", [P, 4], I32)
        w_gcn1 = sb("w_gcn1", [16, 32])
        w_gcn2 = sb("w_gcn2", [32, 16])
        w_gat1 = sb("w_gat1", [16, 96])
        a_gat1 = sb("a_gat1", [16, 2, 96])
        a_gat1w = sb("a_gat1w", [16, 2, 96])
        w_att1 = sb("w_att1", [16, 6])
        w_heads = sb("w_heads", [48, 96])
        w_gat2 = sb("w_gat2", [96, 34])
        a_gat2 = sb("a_gat2", [96, 2, 32])
        w_fin = sb("w_fin", [32, 16])
        w_refl1 = sb("w_refl1", [P, 4, P])
        w_refl2 = sb("w_refl2", [P, 32])
        b_refl1 = sb("b_refl1", [P, 1])
        w_rel1 = sb("w_rel1", [16, REL * 32])
        w_root1 = sb("w_root1", [16, 32])
        w_rel2 = sb("w_rel2", [32, REL * 16])
        w_root2 = sb("w_root2", [32, 16])
        bias = sb("bias", [P, 32 + 16 + 96 + 32 + 16 + 32 + 32 + 16])
        at = [0]

        def bias_at(n):
            at[0] += n
            return bias[:, at[0] - n:at[0]]
        b_gcn1, b_gcn2, b_gat1, b_gat2, b_fin, b_refl2, b_rel1, b_rel2 = [
            bias_at(n) for n in (32, 16, 96, 32, 16, 32, 32, 16)]

        def nodes(tile, f, base=0):
            return tile[:, base:base + NT * f].rearrange("p (t f) -> p t f", f=f)

        block_dst = node_rows[:, 0:NT * BLK].bitcast(I32).rearrange("p (t w) -> p t w", w=BLK)
        block_f = nodes(work, BLK, 3 * COLS - NT * BLK)
        block_le = nodes(scratch, BLK)
        next_of, first_of_last = wide[:, :], not_same_node[:, :]

        rows_at, run_at, spread_at = 0, NB * C * 34, NB * C * (34 + 54)

        def rows_view(b, f):
            o = rows_at + b * C * 34
            return work[:, o:o + C * f].rearrange("p (c f) -> p c f", f=f)

        def run_view(b, w):
            o = run_at + b * C * 54
            return work[:, o:o + C * w].rearrange("p (c f) -> p c f", f=w)

        def spread_view(b, n):
            o = spread_at + b * C * 17
            return work[:, o:o + C * n].rearrange("p (c f) -> p c f", f=n)

        soff = [0]

        def piece(n):
            soff[0] += n
            assert soff[0] <= SCRATCH - P
            return scratch[:, soff[0] - n:soff[0]]

        hist_onehots = [piece(HC * (P + NT) // 2).bitcast(BF16) for _ in range(NB)]
        hist_lo = [h[:, 0:HC * P].rearrange("p (c n) -> p c n", n=P) for h in hist_onehots]
        hist_hi = [h[:, HC * P:HC * (P + NT)].rearrange("p (c n) -> p c n", n=NT) for h in hist_onehots]
        type_onehot = piece(C * REL).rearrange("p (c r) -> p c r", r=REL)
        soff[0] = 0
        score0 = piece(C * 3)
        score1 = piece(C * 3)
        exp_in = piece(C * 6)
        exp_out = piece(C * 6)
        ratio = piece(C * 3)
        gat_msg = piece(C * 48)
        soff[0] = 0
        rel_onehot = piece(C * REL).rearrange("p (c r) -> p c r", r=REL)
        rel_w = piece(C)
        soff[0] = 0
        pair = piece(C * 32).rearrange("p (c f) -> p c f", f=32)
        pair_T = piece(7 * P)
        hidden = [piece(4 * P) for _ in range(2)]
        refl = piece(C * 32)
        prod = piece(C * 32)
        once = piece(C * 32)
        dots = piece(C * 2)
        inv2 = piece(C * 2)
        equal = ends[:, 0:C * P]
        earlier = piece(4 * P)
        src_f = piece(C)
        rank = piece(C)
        fill_dis = piece(C)
        soff[0] = 0

        ps = [ctx.enter_context(nc.psum_tensor(f"ps{i}", [P, 1024], F32)) for i in range(4)]
        ps_T, ps_Y, ps_hist, ps_misc = ps
        ps_lin_T = [ps_T, ps_hist]
        ps_lin_Y = [ps_Y, ps_misc]

        s_dst = sem("s_dst")
        s_loads = sem("s_loads")
        s_zeroed = sem("s_zeroed")
        s_block_idx = sem("s_block_idx")
        s_blocks = sem("s_blocks")
        s_iota = sem("s_iota")
        s_zero_src = sem("s_zero_src")
        s_blk = sem("s_blk")
        s_order = sem("s_order")
        s_hist_ready = [sem(f"s_hist_ready{b}") for b in range(NB)]
        s_hist_used = [sem(f"s_hist_used{b}") for b in range(NB)]
        s_hist_zero = sem("s_hist_zero")
        s_hist_done = sem("s_hist_done")
        s_pe_ask = sem("s_pe_ask")
        s_pe_done = sem("s_pe_done")
        s_act_ask = sem("s_act_ask")
        s_act_done = sem("s_act_done")
        s_rows_stored = sem("s_rows_stored")
        s_rows_ready = sem("s_rows_ready")
        s_rel_ready = sem("s_rel_ready")
        s_rel_stored = sem("s_rel_stored")
        s_idx = [sem(f"s_idx{b}") for b in range(NB)]
        LATER = SHEAF
        s_got_early = [sem(f"s_got_early{b}") for b in range(NB)]
        s_got_later = [sem(f"s_got_later{b}") for b in range(NB)]
        s_run = [sem(f"s_run{b}") for b in range(NB)]
        s_kept = [sem(f"s_kept{b}") for b in range(NB)]
        s_spread_in = [sem(f"s_spread_in{b}") for b in range(NB)]
        s_spread_out = sem("s_spread_out")
        s_first = sem("s_first")
        s_ends = sem("s_ends")
        s_gat_in = sem("s_gat_in")
        s_gat_exp = sem("s_gat_exp")
        s_pair = sem("s_pair")
        s_pair_T = sem("s_pair_T")
        s_pair_S = sem("s_pair_S")
        s_hid = sem("s_hid")
        s_hid_relu = sem("s_hid_relu")
        s_refl = sem("s_refl")
        s_src_row = sem("s_src_row")
        s_msg = sem("s_msg")
        s_src_wide = sem("s_src_wide")
        s_equal = sem("s_equal")
        s_summed = sem("s_summed")
        s_add_ready = [sem(f"s_add_ready{b}") for b in range(NB)]
        s_added = sem("s_added")
        s_lin_in = sem("s_lin_in")
        s_lin_T = sem("s_lin_T")
        s_lin_S = sem("s_lin_S")
        s_lin_out = sem("s_lin_out")
        s_lin_taken = sem("s_lin_taken")
        s_x_in = sem("s_x_in")
        s_x_out = sem("s_x_out")
        s_acc_go = sem("s_acc_go")
        s_acc_in = [sem(f"s_acc_in{u}") for u in range(2)]
        s_acc_used = sem("s_acc_used")
        s_final = sem("s_final")
        s_out = sem("s_out")

        GROUPS4 = (C + 3) // 4
        N_ZERO = sum(SPREAD.values()) + len(acc_tables)
        N_ENDS = 16 * NT
        assert sum(ACC_LOADS) == HALF

        def cols_of(g):
            return min(4, C - 4 * g)

        def tables_stored(engine, k):
            if k in REL_BEFORE:
                engine.wait_ge(s_rel_stored, 16 * NG * REL_BEFORE[k])
            else:
                engine.wait_ge(s_rows_stored, 16 * TABLES_BEFORE[k])

        block = ctx.enter_context(nc.Block())

        @block.sync
        def _(sp):
            loads = [0]

            def load_dst(dst, src, slow=False):
                sp.dma_start(dst, src, allow_slow_non_contiguous=slow).then_inc(s_dst, 16)

            def load(dst, src):
                sp.dma_start(dst, src).then_inc(s_loads, 16)
                loads[0] += 1

            def row(ap):
                return ap.rearrange("(a n) -> a n", a=1)

            dst_pj = A["dst"].rearrange("(p j) -> p j", p=P)
            raw = work[:, :].bitcast(I32)
            load_dst(raw[:, 0:COLS], dst_pj)
            load_dst(bounds[:, 0:1], dst_pj[:, 0:1], slow=True)
            load_dst(bounds[:, 1:2], dst_pj[:, COLS - 1:COLS], slow=True)
            load_dst(bounds[0:P - 1, 2:3], dst_pj[1:P, 0:1], slow=True)
            load_dst(bounds[P - 1:P, 2:3], dst_pj[P - 1:P, COLS - 1:COLS], slow=True)
            load(raw[:, COLS:2 * COLS], A["src"].rearrange("(p j) -> p j", p=P))
            load(raw[:, 2 * COLS:3 * COLS], A["edge_type_8"].rearrange("(p j) -> p j", p=P))
            full = NODES // P
            load(x[:, 0:full, :], A["x"][0:full * P, :].rearrange("(t p) f -> p t f", p=P))
            load(w_gcn1[:, :], A["L0_gnn_W1"])
            load(w_gcn2[:, :], A["L0_gnn_W2"])
            load(w_gat1[:, :], A["L1_gnn_W1"])
            for s, name in enumerate(("L1_gnn_a_src1", "L1_gnn_a_dst1")):
                load(a_gat1[:, s, :], A[name].rearrange("(a h) c -> a (h c)", a=1).partition_broadcast(16))
            load(w_gat2[:, 0:32], A["L1_gnn_W2"])
            for s, name in enumerate(("L1_gnn_a_src2", "L1_gnn_a_dst2")):
                load(a_gat2[:, s, :], A[name].partition_broadcast(96))
            load(w_fin[:, :], A["L1_gnn_Wf"])
            for net in range(2):
                load(b_refl1[64 * net:64 * net + 64, :], A["L2_gnn_b1"].rearrange("(n a) -> n a", a=1))
                load(b_refl2[:, 16 * net:16 * net + 16], row(A["L2_gnn_b2"]).partition_broadcast(P))
            load(w_rel1[:, :], A["L3_gnn_W1"])
            load(w_root1[:, :], A["L3_gnn_root1"])
            load(w_rel2[:, :], A["L3_gnn_W2"])
            load(w_root2[:, :], A["L3_gnn_root2"])
            for tile, name in ((b_gcn1, "L0_gnn_b1"), (b_gcn2, "L0_gnn_b2"), (b_gat1, "L1_gnn_b1"),
                               (b_gat2, "L1_gnn_b2"), (b_fin, "L1_gnn_bf"), (b_rel1, "L3_gnn_b1"),
                               (b_rel2, "L3_gnn_b2")):
                load(tile, row(A[name]).partition_broadcast(P))
            sp.wait_ge(s_zero_src, 1)
            load(x[0:NODES - full * P, full, :], A["x"][full * P:NODES, :])
            assert loads[0] == N_LOADS
            for h in range(3):
                sp.dma_start(w_heads[16 * h:16 * h + 16, 32 * h:32 * h + 32],
                             A["L1_gnn_W1"][:, 32 * h:32 * h + 32]).then_inc(s_blk, 16)
            for net in range(2):
                sp.dma_start(w_refl2[64 * net:64 * net + 64, 16 * net:16 * net + 16],
                             A["L2_gnn_W2"]).then_inc(s_blk, 16)
            for q in range(4):
                for net in range(2):
                    for half in range(2):
                        sp.dma_start(w_refl1[32 * q + 16 * half:32 * q + 16 * half + 16, q, 64 * net:64 * net + 64],
                                     A["L2_gnn_W1"][16 * (half ^ net):16 * (half ^ net) + 16, :]).then_inc(s_blk, 16)
            for b in range(NB):
                sp.sem_inc(s_kept[b], 16)

            def table(n, dst, src):
                sp.wait_ge(s_rows_ready, n + 1)
                sp.dma_start(dst, src).then_inc(s_rows_stored, 16)

            def keep_running(k):
                kept = running[k].rearrange("(p j) w -> p j w", p=P)
                with sp.Fori(0, NIT) as i:
                    for b in range(NB):
                        sp.wait_ge(s_run[b], i + (NIT * k + 1))
                        sp.dma_start(kept[:, bass.ds((i * NB + b) * C, C), :],
                                     run_view(b, RUN_W[k])).then_inc(s_kept[b], 16)

            def whole(t):
                return t.rearrange("(p t) f -> p t f", p=P)

            for k in range(SHEAF + 1):
                table(T_NODE[k], whole(tables[k]), nodes(node_rows, ROW_F[k]))
                keep_running(k)
                if k == GCN1:
                    table(T_INV, whole(inv_table), inv_count[:, :, :])
            sp.wait_ge(s_added, 16 * COLS)
            for b in range(NB):
                sp.wait_ge(s_kept[b], 16 * (NIT * (SHEAF + 1) + 1))
            sp.wait_ge(s_acc_go, 1)
            for n, m in enumerate(ACC_LOADS):
                if n >= 2:
                    sp.wait_ge(s_acc_used, n - 1)
                for q in range(m):
                    o = ((n % 2) * 4 + q) * NT * 16
                    sp.dma_start(work[:, o:o + NT * 16],
                                 acc_tables[sum(ACC_LOADS[:n]) + q][0:ROWS, :].rearrange("(p t) f -> p (t f)", p=P)
                                 ).then_inc(s_acc_in[n % 2], 16)

            def relation_table(n, dst):
                with sp.Fori(0, NG) as g:
                    at_g = bass.ds(g * G, G)
                    sp.wait_ge(s_rel_ready, g + (NG * n + 1))
                    sp.dma_start(dst[:, at_g, :], nodes(work, P)[:, at_g, :]).then_inc(s_rel_stored, 16)

            rel1 = rel1_table.rearrange("(p t r) f -> p t (r f)", p=P, r=REL)
            relation_table(0, rel1[:, :, 0:128])
            relation_table(1, rel1[:, :, 128:256])
            keep_running(REL1)
            relation_table(2, rel2_table.rearrange("(p t r) f -> p t (r f)", p=P, r=REL))
            keep_running(REL2)
            sp.wait_ge(s_final, 1)
            sp.dma_start(out[0:full * P, :].rearrange("(t p) f -> p t f", p=P), x[:, 0:full, :]).then_inc(s_out, 16)
            sp.dma_start(out[full * P:NODES, :], x[0:NODES - full * P, full, :]).then_inc(s_out, 16)
            sp.wait_ge(s_out, 32)

        @block.gpsimd
        def _(pool):
            pool.iota(iota_row[:, :], pattern=[[1, P]], base=0, channel_multiplier=0,
                      allow_small_or_imprecise_dtypes=True).then_inc(s_iota, 1)
            pool.iota(iota_p[:, :], pattern=[[0, 1]], base=0, channel_multiplier=1,
                      allow_small_or_imprecise_dtypes=True).then_inc(s_iota, 1)
            pool.wait_ge(s_block_idx, 1)
            dst_blocks = A["dst"].rearrange("(r w) -> r w", w=BLK)
            for t in range(NT):
                pool.indirect_dma_start(block_dst[:, t, :], None, dst_blocks,
                                        bass.IndirectOffsetOnAxis(ap=block_idx[:, t:t + 1], axis=0)).then_inc(s_blocks, 16)

            def fetch_columns(k, b, columns):
                rows = rows_view(b, ROW_F[k])
                for c in columns:
                    pool.indirect_dma_start(rows[:, c, :], None, gathered[k],
                                            bass.IndirectOffsetOnAxis(ap=idx_chunk[b][:, c:c + 1], axis=0)
                                            ).then_inc((s_got_early if k < LATER else s_got_later)[b], 16)

            def indices_ready(k, b, turn):
                pool.wait_ge(s_idx[b], turn + ((NIT + 1) * k + 1))
                pool.nop(nofuse=True)

            def fetch_chunk(k, b, turn):
                indices_ready(k, b, turn)
                fetch_columns(k, b, range(C))

            def add_columns(b, columns):
                for c in columns:
                    pool.indirect_dma_start(acc_tables[c % HALF], bass.IndirectOffsetOnAxis(ap=add_idx[b][:, c:c + 1], axis=0),
                                            add_rows[b][:, c, :], None, compute_op=ALU.add).then_inc(s_added, 16)

            def add_and_fetch(b, turn, chunk, ahead=None):
                pool.wait_ge(s_add_ready[b], turn + 1)
                pool.nop(nofuse=True)
                add_columns(b, range(0, HALF))
                if ahead:
                    indices_ready(SHEAF, *ahead)
                    fetch_columns(SHEAF, ahead[0], range(0, HALF))
                pool.wait_ge(s_added, chunk * (16 * C) + 16 * HALF)
                pool.nop(nofuse=True)
                add_columns(b, range(HALF, C))
                if ahead:
                    fetch_columns(SHEAF, ahead[0], range(HALF, C))
                pool.wait_ge(s_added, (chunk + 1) * (16 * C))

            def scatter_spread(k):
                n = SPREAD[k]
                src = inv_count[:, :, :] if k == REL1 else nodes(node_rows, ROW_F[k])
                at_lane = SPREAD_AT[k]
                for t in range(NT):
                    pool.indirect_dma_start(spread_rows[k], bass.IndirectOffsetOnAxis(ap=start_idx[:, t:t + 1], axis=0),
                                            src[:, t, at_lane:at_lane + n], None).then_inc(s_spread_out, 16)

            for k in range(7):
                if k in SPREAD and k != REL1:
                    pool.wait_ge(s_rows_ready, T_NODE[k] + 1)
                    scatter_spread(k)
                tables_stored(pool, k)
                if k in SPREAD:
                    table = inv_table if k == REL1 else tables[k]
                    width = REL if k == REL1 else ROW_F[k]
                    pool.indirect_dma_start(first_row[:, 0:width], None, table,
                                            bass.IndirectOffsetOnAxis(ap=first_idx[:, 0:1], axis=0)).then_inc(s_first, 16)
                if k != SHEAF:
                    with pool.Fori(0, NIT) as i:
                        for b in range(NB):
                            fetch_chunk(k, b, i)
                else:
                    AHEAD = 3
                    for b in range(AHEAD):
                        fetch_chunk(k, b, 0)
                    with pool.Fori(0, NIT - 1) as i:
                        for b in range(NB):
                            add_and_fetch(b, i, i * NB + b, ((b + AHEAD) % NB, i + (b + AHEAD) // NB))
                    for b in range(NB):
                        add_and_fetch(b, NIT - 1, NB * (NIT - 1) + b, (b + AHEAD, NIT - 1) if b + AHEAD < NB else None)
                for b in range(NB):
                    pool.wait_ge(s_kept[b], 16 * (NIT * (k + 1) + 1))
                if k == GCN1:
                    pool.wait_ge(s_zeroed, 16 * N_ZERO)
                w = RUN_W[k]
                for t in range(NT):
                    pool.indirect_dma_start(nodes(ends, w)[:, t, :], None, running[k],
                                            bass.IndirectOffsetOnAxis(ap=end_idx[:, t:t + 1], axis=0)).then_inc(s_ends, 16)
                if k == GCN1:
                    pool.wait_ge(s_rows_ready, T_INV + 1)
                    scatter_spread(REL1)

        @block.scalar
        def _(act):
            asked = [0]
            lin = [0]

            def node_function(dst, src, func, **more):
                asked[0] += 1
                act.wait_ge(s_act_ask, asked[0])
                nc.scalar.activation(dst, src, func, **more).then_inc(s_act_done, 1)

            def linear(fi):
                base = NG * lin[0]
                lin[0] += 1
                with act.Fori(0, NG // 2) as i:
                    for u in range(2):
                        act.wait_ge(s_lin_T, i * 2 + (base + u + 1))
                        nc.scalar.activation(staged_T[u][0:fi, :], ps_lin_T[u][0:fi, 0:G * P], ACT.Copy).then_inc(s_lin_S, 1)

            def load_spread(k, b, i):
                e = SPREAD_NO[k]
                act.wait_ge(s_idx[b], i + ((NIT + 1) * k + 1))
                act.dma_start(spread_view(b, SPREAD[k]),
                              spread_rows[k][0:EDGES, :].rearrange("(p j) n -> p j n", p=P)[:, bass.ds((i * NB + b) * C, C), :]
                              ).then_inc(s_spread_in[b], 16)

            def spread_landed(k):
                act.wait_ge(s_spread_out, N_ENDS * SCATTERED[k])

            def gat_pass(k):
                spread_landed(k)
                n = 2 * HEADS[k] * C
                with act.Fori(0, NIT) as i:
                    for b in range(NB):
                        load_spread(k, b, i)
                        act.wait_ge(s_gat_in, (i * NB + b) + (NCH * (k - GAT1) + 1))
                        nc.scalar.activation(exp_out[:, 0:n], exp_in[:, 0:n], ACT.Exp).then_inc(s_gat_exp, 1)

            def sheaf_pass():
                spread_landed(SHEAF)
                with act.Fori(0, NIT) as i:
                    for b in range(NB):
                        c = i * NB + b
                        load_spread(SHEAF, b, i)
                        act.wait_ge(s_pair_T, c + 1)
                        nc.scalar.activation(pair_T[:, 0:6 * P], ps_T[:, 0:6 * P], ACT.Copy)
                        nc.scalar.activation(pair_T[0:32, 6 * P:7 * P], ps_T[0:32, 6 * P:7 * P], ACT.Copy).then_inc(s_pair_S, 1)
                        for g in range(GROUPS4):
                            n = cols_of(g) * P
                            act.wait_ge(s_hid, c * GROUPS4 + (g + 1))
                            if g >= 2:
                                act.wait_ge(s_refl, c * GROUPS4 + (g - 1))
                            nc.scalar.activation(hidden[g % 2][:, 0:n], ps_hist[:, 512 * (g % 2):512 * (g % 2) + n],
                                                 ACT.Relu, bias=b_refl1[:, 0:1]).then_inc(s_hid_relu, 1)

            node_function(small[:, 1, :], small[:, 0, :], ACT.Sqrt)
            node_function(small[:, 1, :], small[:, 0, :], ACT.Sqrt)
            per_p = (EDGES + P) // P
            per_acc = (ROWS + P) // P * 16
            cleared = []
            for k, n in SPREAD.items():
                flat = spread_rows[k].rearrange("(p a) n -> p (a n)", p=P)
                cleared += [flat[:, l * per_p:(l + 1) * per_p] for l in range(n)]
            cleared += [acc.rearrange("(p a) f -> p (a f)", p=P) for acc in acc_tables]
            assert len(cleared) == N_ZERO
            for n, dst in enumerate(cleared):
                if n % 2 == 0:
                    act.wait_ge(s_idx[0], n // 2 + 2)
                act.dma_start(dst, ends[:, 0:dst.shape[1]]).then_inc(s_zeroed, 16)
            linear(16)
            linear(32)
            node_function(small[:, 1, :], small[:, 0, :], ACT.Sqrt)
            linear(16)
            gat_pass(GAT1)
            node_function(tail_m[:, 3:6], tail_m[:, 3:6], ACT.Exp)
            merge = work[:, 9408:9408 + 9 * NT]
            node_function(merge, merge, ACT.Exp)
            linear(48)
            for _ in range(2):
                node_function(scratch[:, 0:48 * NT], scratch[:, 0:48 * NT], ACT.Exp)
            linear(96)
            gat_pass(GAT2)
            node_function(tail_m[:, 3:4], tail_m[:, 3:4], ACT.Exp)
            merge = work[:, 9408:9408 + 3 * NT]
            node_function(merge, merge, ACT.Exp)
            node_function(scratch[:, 0:32 * NT], scratch[:, 0:32 * NT], ACT.Exp)
            linear(32)
            node_function(small[:, 1, :], small[:, 0, :], ACT.Sqrt)
            node_function(small[:, 1, :], small[:, 0, :], ACT.Sqrt)
            sheaf_pass()
            node_function(small[:, 1, :], small[:, 0, :], ACT.Sqrt)
            linear(16)
            linear(16)
            linear(16)
            spread_landed(REL1)
            with act.Fori(0, NIT) as i:
                for b in range(NB):
                    load_spread(REL1, b, i)
            linear(32)
            linear(32)

        @block.tensor
        def _(pe):
            asked = [0]
            lin = [0]
            xtr = [0]
            zero_bf = scratch[:, SCRATCH - P:SCRATCH].bitcast(BF16)

            def count(kh, turns, before):
                pe.wait_ge(s_hist_zero, kh + 1)
                nc.tensor.matmul(ps_hist[:, 0:NT], zero_bf[:, 0:P], zero_bf[:, 0:NT], start=True, stop=False, skip_group_check=True)
                with pe.Fori(0, turns) as i:
                    for b in range(NB):
                        pe.wait_ge(s_hist_ready[b], i + (before + 1))
                        for c in range(HC):
                            last = nc.tensor.matmul(ps_hist[:, 0:NT], hist_lo[b][:, c, :], hist_hi[b][:, c, :],
                                                    start=False, stop=False, skip_group_check=True)
                        last.then_inc(s_hist_used[b], 1)
                nc.tensor.matmul(ps_hist[:, 0:NT], zero_bf[:, 0:P], zero_bf[:, 0:NT], start=False, stop=True,
                                 skip_group_check=True).then_inc(s_hist_done, 1)

            def single(dst, lhsT, rhs):
                asked[0] += 1
                pe.wait_ge(s_pe_ask, asked[0])
                nc.tensor.matmul(dst, lhsT, rhs, start=True, stop=True).then_inc(s_pe_done, 1)

            def linear(fi, fo, w):
                base = NG * lin[0]
                lin[0] += 1

                def transpose(u, g):
                    pe.wait_ge(s_lin_in, g + (base + 1))
                    pe.nop(nofuse=True)
                    for t in range(G):
                        last = nc.tensor.transpose(ps_lin_T[u][0:fi, t * P:(t + 1) * P], stages[u][:, t, 0:fi], ident[:, :])
                    last.then_inc(s_lin_T, 1)

                def product(u, g):
                    pe.wait_ge(s_lin_S, g + (base + 1))
                    pe.wait_ge(s_lin_taken, g + (base + 1))
                    for t in range(G):
                        last = nc.tensor.matmul(ps_lin_Y[u][:, t * P:t * P + fo], staged_T[u][0:fi, t * P:(t + 1) * P], w,
                                                start=True, stop=True)
                    last.then_inc(s_lin_out, 1)

                transpose(0, 0)
                with pe.Fori(0, NG // 2 - 1) as i:
                    for u in range(2):
                        transpose(1 - u, i * 2 + (u + 1))
                        product(u, i * 2 + u)
                transpose(1, NG - 1)
                product(0, NG - 2)
                product(1, NG - 1)

            def extras(w):
                base = NG * xtr[0]
                xtr[0] += 1
                with pe.Fori(0, NG) as g:
                    pe.wait_ge(s_x_in, g + (base + 1))
                    nc.tensor.matmul(ps_misc[:, 0:G * w], onehot_p[:, :], stages[0][:, :, :].rearrange("p g f -> p (g f)")[:, 0:G * w],
                                     start=True, stop=True).then_inc(s_x_out, 1)

            def sheaf_pass():
                pairs = pair.rearrange("p c f -> p (c f)")
                with pe.Fori(0, NCH) as c:
                    pe.wait_ge(s_pair, c + 1)
                    for g in range(GROUPS4):
                        n = 32 * cols_of(g)
                        last = nc.tensor.transpose(ps_T[0:n, g * P:(g + 1) * P], pairs[:, 128 * g:128 * g + n], ident[:, :])
                    last.then_inc(s_pair_T, 1)

                    def src_wide(g):
                        for u in range(cols_of(g)):
                            last = nc.tensor.matmul(ps_misc[:, u * P:(u + 1) * P],
                                                    src_f[:, 4 * g + u:4 * g + u + 1].to_broadcast([P, P]), ident[:, :],
                                                    start=True, stop=True)
                        last.then_inc(s_src_wide, 1)

                    pe.wait_ge(s_src_row, c + 1)
                    src_wide(0)
                    pe.wait_ge(s_pair_S, c + 1)

                    def second_layer(g):
                        pe.wait_ge(s_hid_relu, c * GROUPS4 + (g + 1))
                        for u in range(cols_of(g)):
                            col = 4 * g + u
                            last = nc.tensor.matmul(ps_Y[:, 32 * col:32 * col + 32], hidden[g % 2][:, u * P:(u + 1) * P],
                                                    w_refl2[:, :], start=True, stop=True)
                        last.then_inc(s_refl, 1)

                    for g in range(GROUPS4):
                        kk = 32 * cols_of(g)
                        for u in range(cols_of(g)):
                            last = nc.tensor.matmul(ps_hist[:, 512 * (g % 2) + u * P:512 * (g % 2) + (u + 1) * P],
                                                    w_refl1[0:kk, u, :], pair_T[0:kk, g * P:(g + 1) * P],
                                                    start=True, stop=True)
                        last.then_inc(s_hid, 1)
                        if g >= 1:
                            second_layer(g - 1)
                            pe.wait_ge(s_equal, c * GROUPS4 + g)
                            src_wide(g)
                    second_layer(GROUPS4 - 1)
                    pe.wait_ge(s_msg, c + 1)
                    for col in range(C):
                        last = nc.tensor.matmul(ps_misc[:, 512 + 16 * col:512 + 16 * col + 16],
                                                equal[:, col * P:(col + 1) * P], once[:, 32 * col:32 * col + 16],
                                                start=True, stop=True)
                    last.then_inc(s_summed, 1)

            for b in range(NB):
                pe.sem_inc(s_hist_used[b], 1)
            pe.sem_inc(s_lin_taken, 2)
            count(0, SAMPLES // C, 0)
            single(ps_misc[:, 0:NT], upto[:, :], small[:, 0, :])
            single(ps_misc[:, P:P + NT], ones[:, :], small[:, 0, :])
            single(ps_misc[:, 0:NT], next_of[:, :], small[:, 2, :])
            single(ps_misc[:, P:P + NT], first_of_last[:, :], small[:, 3, :])
            single(ps_misc[:, 512:512 + P], wide[:, :], ident[:, :])
            count(1, NCH, SAMPLES // C)
            extras(RUN_W[GCN1])
            linear(16, 32, w_gcn1[:, :])
            linear(32, 16, w_gcn2[:, :])
            extras(RUN_W[GCN2])
            linear(16, 6, w_att1[:, :])
            for h in range(3):
                single(ps_misc[:, 512:512 + P], wide[:, :], ident[:, :])
            extras(RUN_W[GAT1] + 1)
            linear(48, 96, w_heads[:, :])
            linear(96, 34, w_gat2[:, :])
            single(ps_misc[:, 512:512 + P], wide[:, :], ident[:, :])
            extras(RUN_W[GAT2] + 1)
            linear(32, 16, w_fin[:, :])
            sheaf_pass()
            extras(RUN_W[SHEAF])
            linear(16, 128, w_rel1[:, 0:128])
            linear(16, 128, w_rel1[:, 128:256])
            linear(16, 32, w_root1[:, :])
            extras(RUN_W[REL1])
            linear(32, 128, w_rel2[:, :])
            linear(32, 16, w_root2[:, :])
            extras(RUN_W[REL2])

        @block.vector
        def _(v):
            V = nc.vector
            step = [0]

            def then(ins):
                step[0] += 1
                ins.then_inc(s_order, 1)
                v.wait_ge(s_order, step[0])
                return ins

            def fresh():
                v.sem_clear(s_order)
                step[0] = 0

            def tt(o, a, b, op):
                return V.tensor_tensor(o, a, b, op)

            def ts(o, a, s1, s2, op0, op1=None):
                if op1 is None:
                    return V.tensor_scalar(o, a, s1, None, op0)
                return V.tensor_scalar(o, a, s1, s2, op0, op1)

            def bc_last(ap, n):
                return ap.unsqueeze(len(ap.shape)).to_broadcast(list(ap.shape) + [n])

            def bc_mid(ap, n):
                return ap.unsqueeze(1).to_broadcast([ap.shape[0], n] + list(ap.shape[1:]))

            asks = {"pe": 0, "act": 0}

            def tell_act():
                asks["act"] += 1
                v.sem_inc(s_act_ask, 1)

            def hear_act():
                v.wait_ge(s_act_done, asks["act"])

            def ask_act():
                tell_act()
                hear_act()

            def ask_pe(n=1):
                asks["pe"] += n
                v.sem_inc(s_pe_ask, n)
                v.wait_ge(s_pe_done, asks["pe"])

            def inverse_sqrt(dst):
                ask_act()
                then(V.reciprocal(dst, small[:, 1, :]))

            def layer_norm():
                sq = nodes(scratch, 16)
                then(V.tensor_reduce(small[:, 2, :], x[:, :, :], AX.X, ALU.add))
                then(ts(small[:, 2, :], small[:, 2, :], 1.0 / 16, None, ALU.mult))
                then(tt(hn[:, :, :], x[:, :, :], bc_last(small[:, 2, :], 16), ALU.subtract))
                then(tt(sq, hn[:, :, :], hn[:, :, :], ALU.mult))
                then(V.tensor_reduce(small[:, 2, :], sq, AX.X, ALU.add))
                then(ts(small[:, 0, :], small[:, 2, :], 1.0 / 16, EPS, ALU.mult, ALU.add))
                inverse_sqrt(small[:, 3, :])
                then(tt(hn[:, :, :], hn[:, :, :], bc_last(small[:, 3, :], 16), ALU.mult))
                then(ts(hn[:, :, :], hn[:, :, :], 0.0, None, ALU.max))

            lin = [0]
            xtr = [0]

            def linear(dst, src, fi, fo, bias=None, relations=None):
                base = NG * lin[0]
                lin[0] += 1

                def put(u, g):
                    V.tensor_copy(stages[u][:, :, 0:fi], src[:, bass.ds(g * G, G), :]).then_inc(s_lin_in, 1)

                def put_next(u, g):
                    v.wait_ge(s_lin_T, g + (base - 1))
                    v.nop(nofuse=True)
                    put(u, g)

                def take(u, g):
                    v.wait_ge(s_lin_out, g + (base + 1))
                    v.nop(nofuse=True)
                    y = ps_lin_Y[u][:, 0:G * P].rearrange("p (g f) -> p g f", f=P)[:, :, 0:fo]
                    if bias is None:
                        then(V.tensor_copy(dst[:, bass.ds(g * G, G), :], y))
                    else:
                        then(tt(dst[:, bass.ds(g * G, G), :], y, bc_mid(bias, G), ALU.add))
                    v.sem_inc(s_lin_taken, 1)
                    if relations is not None:
                        v.sem_inc(s_rel_ready, 1)

                put(0, 0)
                put(1, 1)
                if relations == 1:
                    v.wait_ge(s_rel_stored, 16 * NG)
                with v.Fori(0, NG // 2 - 1) as i:
                    fresh()
                    for u in range(2):
                        put_next(u, i * 2 + (u + 2))
                        take(u, i * 2 + u)
                take(0, NG - 2)
                take(1, NG - 1)

            def extras(w):
                base = NG * xtr[0]
                xtr[0] += 1
                dst = nodes(scratch, w)
                op = stages[0][:, :, :].rearrange("p g f -> p (g f)")[:, 0:G * w].rearrange("p (g f) -> p g f", f=w)
                with v.Fori(0, NG) as g:
                    fresh()
                    tt(op, bc_last(onehot_t[:, bass.ds(g * G, G)], w), bc_mid(tail[:, 0:w], G), ALU.mult).then_inc(s_x_in, 1)
                    v.wait_ge(s_x_out, g + (base + 1))
                    v.nop(nofuse=True)
                    then(V.tensor_copy(dst[:, bass.ds(g * G, G), :], ps_misc[:, 0:G * w].rearrange("p (g f) -> p g f", f=w)))
                return dst

            def pass_done(k):
                w = RUN_W[k]
                v.wait_ge(s_run[NB - 1], NIT * (k + 1))
                for b in range(NB):
                    v.wait_ge(s_kept[b], 16 * (NIT * (k + 1) + 1))
                then(V.tensor_copy(tail[:, 0:w], run_view(NB - 1, w)[:, C - 1, :]))

            def ends_in(k):
                v.wait_ge(s_ends, N_ENDS * (k + 1))
                return nodes(ends, RUN_W[k])

            def summed(k):
                w = RUN_W[k]
                pass_done(k)
                more = extras(w)
                total = ends_in(k)
                then(tt(total, total, bc_last(has[:, :], w), ALU.mult))
                then(tt(total, total, more, ALU.add))
                return total

            def selu(z, f):
                e = nodes(scratch, f)
                then(ts(e, z, 0.0, None, ALU.min))
                tell_act()
                then(ts(z, z, 0.0, SELU_S, ALU.max, ALU.mult))
                hear_act()
                then(ts(e, e, SELU_S * SELU_A, -SELU_S * SELU_A, ALU.mult, ALU.add))
                then(tt(z, z, e, ALU.add))

            def gat_nodes(k):
                heads, d, w = HEADS[k], HEAD_D[k], RUN_W[k]
                o, m0 = heads * d, heads * d + heads
                pass_done(k)
                for h in range(heads):
                    then(V.tensor_copy(wide[:, :], tail[:, m0 + h:m0 + h + 1].to_broadcast([P, P])))
                    ask_pe()
                    then(tt(wide[:, :], ps_misc[:, 512:512 + P], not_same_node[:, :], ALU.add))
                    then(V.tensor_reduce(tail_m[:, h:h + 1], wide[:, :], AX.X, ALU.max))
                then(tt(tail_m[:, 3:3 + heads], tail[:, m0:m0 + heads], tail_m[:, 0:heads], ALU.subtract))
                then(ts(tail_m[:, 3:3 + heads], tail_m[:, 3:3 + heads], 0.0, None, ALU.min))
                ask_act()
                for h in range(heads):
                    ts(tail[:, h * d:(h + 1) * d], tail[:, h * d:(h + 1) * d], tail_m[:, 3 + h:4 + h], None, ALU.mult)
                then(tt(tail[:, o:o + heads], tail[:, o:o + heads], tail_m[:, 3:3 + heads], ALU.mult))
                ts(tail[:, m0:m0 + heads], tail_m[:, 0:heads], rep[:, 0:1], None, ALU.mult)
                then(V.tensor_copy(tail[:, w:w + 1], rep[:, 0:1]))
                more = extras(w + 1)
                end = ends_in(k)
                merge = work[:, 9408:9408 + 3 * heads * NT].rearrange("p (s t h) -> p s t h", s=3, h=heads)
                top = work[:, 9408 + 9 * NT:9408 + (9 + heads) * NT].rearrange("p (t h) -> p t h", h=heads)
                tot = work[:, 9408 + 12 * NT:9408 + (12 + heads) * NT].rearrange("p (t h) -> p t h", h=heads)
                att = nodes(node_rows, ROW_F[k])
                own, tails, loop = merge[:, 0], merge[:, 1], merge[:, 2]
                ts(small[:, 0, :], has[:, :], -1.0, BIG, ALU.add, ALU.mult)
                then(ts(small[:, 1, :], more[:, :, w], -1.0, BIG, ALU.add, ALU.mult))
                tt(own, end[:, :, m0:m0 + heads], bc_last(has[:, :], heads), ALU.mult)
                tt(tails, more[:, :, m0:m0 + heads], bc_last(small[:, 1, :], heads), ALU.add)
                then(tt(loop, att[:, :, d:d + heads], att[:, :, d + heads:d + 2 * heads], ALU.add))
                then(tt(own, own, bc_last(small[:, 0, :], heads), ALU.add))
                then(V.scalar_tensor_tensor(tot, loop, SLOPE, loop, ALU.mult, ALU.max))
                then(V.tensor_copy(loop, tot))
                then(tt(top, own, tails, ALU.max))
                then(tt(top, top, loop, ALU.max))
                for part in (own, tails, loop):
                    last = tt(part, part, top, ALU.subtract)
                then(last)
                ask_act()
                then(tt(tot, end[:, :, o:o + heads], own, ALU.mult))
                then(tt(top, more[:, :, o:o + heads], tails, ALU.mult))
                then(tt(tot, tot, top, ALU.add))
                then(tt(tot, tot, loop, ALU.add))
                then(ts(tot, tot, 1e-16, None, ALU.add))
                then(V.reciprocal(top, tot))
                for part in (own, tails, loop):
                    last = tt(part, part, top, ALU.mult)
                then(last)
                self_rows = hn[:, :, :] if k == GAT1 else att[:, :, 0:d]
                part = work[:, 0:NT * d].rearrange("p (t f) -> p t f", f=d)
                for h in range(heads):
                    of = end[:, :, h * d:(h + 1) * d]
                    then(tt(of, of, bc_last(own[:, :, h], d), ALU.mult))
                    then(tt(part, more[:, :, h * d:(h + 1) * d], bc_last(tails[:, :, h], d), ALU.mult))
                    then(tt(of, of, part, ALU.add))
                    then(tt(part, self_rows, bc_last(loop[:, :, h], d), ALU.mult))
                    then(tt(of, of, part, ALU.add))
                return end[:, :, 0:o]

            def hand_indices(k, b, c):
                at_c = bass.ds(c * C, C)
                if k < REL1:
                    V.tensor_copy(idx_chunk[b][:, :], row_of_src[:, at_c]).then_inc(s_idx[b], 1)
                else:
                    V.scalar_tensor_tensor(idx_chunk[b][:, :], row_of_src[:, at_c], float(REL), etype[:, at_c],
                                           ALU.mult, ALU.add).then_inc(s_idx[b], 1)

            def scans(k, b, lanes, carry_on, values, start=0):
                cur, prev = run_view(b, RUN_W[k]), run_view((b - 1) % NB, RUN_W[k])
                for f in range(lanes):
                    last = V.tensor_tensor_scan(cur[:, :, start + f], carry_on, values[:, :, f],
                                                prev[:, C - 1, start + f:start + f + 1], ALU.mult, ALU.add)
                return last

            def count_step(c, before):
                for b in range(NB):
                    v.wait_ge(s_hist_used[b], c + (before + 1))
                    cc = bass.ds(c * C + b * HC, HC)
                    tt(hist_lo[b], bc_last(lo_all[:, cc], P), bc_mid(iota_bf[:, :], HC), ALU.is_equal)
                    tt(hist_hi[b], bc_last(hi_all[:, cc], NT), bc_mid(iota_bf[:, 0:NT], HC), ALU.is_equal).then_inc(s_hist_ready[b], 1)

            def spread_values(k, b, i, into=None):
                n = SPREAD[k]
                sv = spread_view(b, n)
                v.wait_ge(s_spread_in[b], (i + (NIT * SPREAD_NO[k] + 1)) * 16)
                then(tt(sv, sv, bc_last(start_c[:, :], n), ALU.mult))
                for f in range(n):
                    dst = sv[:, :, f] if into is None else into(f)
                    last = V.tensor_tensor_scan(dst, same_c[:, :], sv[:, :, f], carry[:, f:f + 1], ALU.mult, ALU.add)
                then(last)
                if into is None:
                    then(V.tensor_copy(carry[:, 0:n], sv[:, C - 1, :]))
                return sv

            def edge_chunk(k, i, b):
                c = i * NB + b
                at_c = bass.ds(c * C, C)
                w, f_in = RUN_W[k], ROW_F[k]
                rows, run, prev = rows_view(b, f_in), run_view(b, w), run_view((b - 1) % NB, w)
                V.tensor_copy(same_c[:, :], same[:, at_c])
                then(ts(start_c[:, :], same[:, at_c], -1.0, 1.0, ALU.mult, ALU.add))
                if k == GCN1:
                    then(tt(type_onehot, bc_last(etype[:, at_c], REL), bc_mid(iota_bf[:, 0:REL], C), ALU.is_equal))
                    count_step(c, SAMPLES // C)
                if k == REL1:
                    spread = spread_values(k, b, i)
                    then(tt(rel_onehot, bc_last(etype[:, at_c], REL), bc_mid(iota_bf[:, 0:REL], C), ALU.is_equal))
                    then(tt(rel_onehot, rel_onehot, spread, ALU.mult))
                    then(V.tensor_reduce(rel_w, rel_onehot, AX.X, ALU.add))
                    V.tensor_copy(edge_weight[:, at_c], rel_w)
                if k == REL2:
                    then(V.tensor_copy(rel_w, edge_weight[:, at_c]))
                if k in HEADS:
                    spread = spread_values(k, b, i)
                    then(ts(neg_c[:, :], same_c[:, :], -1.0, BIG, ALU.add, ALU.mult))
                if k < LATER:
                    v.wait_ge(s_got_early[b], (i + (NIT * k + 1)) * (16 * C))
                else:
                    v.wait_ge(s_got_later[b], (i + (NIT * (k - LATER) + 1)) * (16 * C))
                v.wait_ge(s_kept[b], (i + (NIT * k + 1)) * 16)
                if k == GCN1:
                    scans(k, b, 16, same_c[:, :], rows)
                    last = scans(k, b, REL, same_c[:, :], type_onehot, 16)
                elif k == GCN2:
                    last = scans(k, b, 16, same_c[:, :], rows)
                elif k in (REL1, REL2):
                    then(tt(rows, rows, bc_last(rel_w, f_in), ALU.mult))
                    last = scans(k, b, w, same_c[:, :], rows)
                elif k in HEADS:
                    heads, d = HEADS[k], HEAD_D[k]
                    o, m0 = heads * d, heads * d + heads
                    lanes = lambda t, n: t[:, 0:C * n].rearrange("p (c h) -> p c h", h=n)
                    raw, score, ein, eout, rat = lanes(score0, heads), lanes(score1, heads), lanes(exp_in, 2 * heads), \
                        lanes(exp_out, 2 * heads), lanes(ratio, heads)
                    msg = lanes(gat_msg, o)
                    then(tt(raw, rows[:, :, d:d + heads], spread, ALU.add))
                    then(V.scalar_tensor_tensor(score, raw, SLOPE, raw, ALU.mult, ALU.max))
                    for h in range(heads):
                        last = V.tensor_tensor_scan(run[:, :, m0 + h], neg_c[:, :], score[:, :, h],
                                                    prev[:, C - 1, m0 + h:m0 + h + 1], ALU.add, ALU.max)
                    then(last)
                    mx = run[:, :, m0:m0 + heads]
                    tt(ein[:, 1:C, 0:heads], mx[:, 0:C - 1, :], mx[:, 1:C, :], ALU.subtract)
                    tt(ein[:, 0, 0:heads], prev[:, C - 1, m0:m0 + heads], mx[:, 0, :], ALU.subtract)
                    then(tt(ein[:, :, heads:2 * heads], score, mx, ALU.subtract))
                    ts(ein, ein, 0.0, None, ALU.min).then_inc(s_gat_in, 1)
                    v.wait_ge(s_gat_exp, c + (NCH * (k - GAT1) + 1))
                    tt(rat, eout[:, :, 0:heads], bc_last(same_c[:, :], heads), ALU.mult)
                    for h in range(heads):
                        last = tt(msg[:, :, h * d:(h + 1) * d], rows[:, :, 0:d], bc_last(eout[:, :, heads + h], d), ALU.mult)
                    then(last)
                    for h in range(heads):
                        scans(k, b, d, rat[:, :, h], msg[:, :, h * d:(h + 1) * d], h * d)
                        last = scans(k, b, 1, rat[:, :, h], eout[:, :, heads + h:heads + h + 1], o + h)
                else:
                    last = sheaf_chunk(i, b, c, rows)
                then(last)
                v.sem_inc(s_run[b], 1)
                hand_indices(k, b, c + NB)

            def sheaf_chunk(i, b, c, rows):
                as32 = lambda t: t.rearrange("p (c f) -> p c f", f=32)
                as2 = lambda t: t.rearrange("p (c s f) -> p (c s) f", s=2, f=16)
                vec, pr, y = as32(refl), as32(prod), as32(once)
                flat = pair.rearrange("p c f -> p (c f)")
                V.tensor_copy(pair[:, :, 0:16], rows[:, :, 0:16])
                then(V.tensor_copy(src_f, row_of_src[:, bass.ds(c * C, C)]))
                v.sem_inc(s_src_row, 1)
                sv = spread_values(SHEAF, b, i, lambda f: pair[:, :, 16 + f] if f < 16 else fill_dis)
                V.tensor_copy(carry[:, 0:16], pair[:, C - 1, 16:32])
                then(V.tensor_copy(carry[:, 16:17], fill_dis[:, C - 1:C]))
                v.sem_inc(s_pair, 1)

                def equality(g):
                    n = cols_of(g)
                    v.wait_ge(s_src_wide, c * GROUPS4 + (g + 1))
                    eq = equal[:, 4 * g * P:(4 * g + n) * P].rearrange("p (u q) -> p u q", q=P)
                    before = earlier[:, 0:n * P].rearrange("p (u q) -> p u q", q=P)
                    then(tt(eq, ps_misc[:, 0:n * P].rearrange("p (u q) -> p u q", q=P),
                            bc_last(src_f[:, 4 * g:4 * g + n], P), ALU.is_equal))
                    v.sem_inc(s_equal, 1)
                    then(tt(before, eq, bc_mid(below[:, :], n), ALU.mult))
                    then(V.tensor_reduce(rank[:, 4 * g:4 * g + n], before, AX.X, ALU.add))

                for g in range(GROUPS4):
                    equality(g)
                then(ts(rank, rank, 0.5, None, ALU.is_lt))
                then(ts(src_f, src_f, spare_node[:, 0:1], None, ALU.subtract))
                then(tt(src_f, src_f, rank, ALU.mult))
                ts(add_idx[b][:, :], src_f, spare_node[:, 0:1], None, ALU.add)
                v.wait_ge(s_refl, (c + 1) * GROUPS4)
                then(tt(vec, ps_Y[:, 0:C * 32].rearrange("p (c f) -> p c f", f=32), bc_mid(b_refl2, C), ALU.add))
                tt(pr, vec, vec, ALU.mult)
                then(tt(y, vec, pair, ALU.mult))
                V.tensor_reduce(inv2, as2(prod), AX.X, ALU.add)
                then(V.tensor_reduce(dots, as2(once), AX.X, ALU.add))
                then(ts(inv2, inv2, 1e-24, None, ALU.max))
                then(V.reciprocal(inv2, inv2))
                then(V.scalar_tensor_tensor(dots, dots, 2.0, inv2, ALU.mult, ALU.mult))
                then(tt(as2(prod), as2(refl), bc_last(dots, 16), ALU.mult))
                tt(y[:, :, 0:16], pair[:, :, 16:32], pr[:, :, 16:32], ALU.subtract)
                then(tt(y[:, :, 16:32], pair[:, :, 0:16], pr[:, :, 0:16], ALU.subtract))
                then(tt(pr, vec, y, ALU.mult))
                then(V.tensor_reduce(dots, as2(prod), AX.X, ALU.add))
                then(V.scalar_tensor_tensor(dots, dots, 2.0, inv2, ALU.mult, ALU.mult))
                then(tt(as2(prod), as2(refl), bc_last(dots, 16), ALU.mult))
                then(tt(y, y, pr, ALU.subtract))
                tt(y[:, :, 0:16], y[:, :, 0:16], bc_last(fill_dis, 16), ALU.mult)
                then(tt(y[:, :, 16:32], y[:, :, 16:32], bc_last(rows[:, :, 16], 16), ALU.mult))
                v.sem_inc(s_msg, 1)
                last = scans(SHEAF, b, 16, same_c[:, :], y[:, :, 16:32])
                v.wait_ge(s_summed, c + 1)
                V.tensor_copy(add_rows[b][:, :, :], ps_misc[:, 512:512 + C * 16].rearrange("p (c f) -> p c f", f=16)).then_inc(s_add_ready[b], 1)
                return last

            def boundaries():
                lo_hi_i = bounds_lohi[:, :]
                then(split(lo_hi_i[:, 0:2], bounds[:, 0:2], ALU.bitwise_and, P - 1))
                then(split(lo_hi_i[:, 2:4], bounds[:, 0:2], ALU.logical_shift_right, 7))
                then(V.tensor_copy(bnd[:, 0:4], lo_hi_i))
                then(V.tensor_copy(bnd[:, 4:6], bounds[:, 1:3]))
                then(V.scalar_tensor_tensor(first_idx[:, :], bnd[:, 0:1], float(NT), bnd[:, 2:3], ALU.mult, ALU.add))
                then(tt(bnd[:, 6:7], bnd[:, 4:5], bnd[:, 5:6], ALU.is_equal))
                then(ts(bnd[:, 7:8], iota_p[:, :], P - 1.5, None, ALU.is_lt))
                then(tt(bnd[:, 6:7], bnd[:, 6:7], bnd[:, 7:8], ALU.mult))
                then(ts(onehot_p[:, :], iota_row[:, :], bnd[:, 1:2], bnd[:, 6:7], ALU.is_equal, ALU.mult))
                then(ts(onehot_t[:, :], iota_row[:, 0:NT], bnd[:, 3:4], None, ALU.is_equal))
                then(ts(bnd[:, 8:9], bnd[:, 4:5], 1.0, None, ALU.add))
                then(tt(bnd[:, 8:9], bnd[:, 8:9], bnd[:, 6:7], ALU.mult))
                then(V.tensor_copy(wide[:, :], bnd[:, 8:9].to_broadcast([P, P])))
                ask_pe()
                then(ts(bnd[:, 9:10], bnd[:, 4:5], 1.0, None, ALU.add))
                then(ts(wide[:, :], ps_misc[:, 512:512 + P], bnd[:, 9:10], None, ALU.is_equal))
                ts(not_same_node[:, :], wide[:, :], -1.0, BIG, ALU.add, ALU.mult)
                then(tt(wide[:, :], wide[:, :], below[:, :], ALU.mult))
                then(V.tensor_reduce(bnd[:, 10:11], wide[:, :], AX.X, ALU.add))
                then(ts(rep[:, :], bnd[:, 10:11], 0.5, bnd[:, 6:7], ALU.is_lt, ALU.mult))
                for s in range(2):
                    then(tt(a_gat1w[:, s, :], w_gat1[:, :], a_gat1[:, s, :], ALU.mult))
                    then(V.tensor_reduce(w_att1[:, 3 * s:3 * s + 3], a_gat1w[:, s, :].rearrange("p (h c) -> p h c", c=32), AX.X, ALU.add))
                    then(tt(a_gat2[:, s, :], w_gat2[:, 0:32], a_gat2[:, s, :], ALU.mult))
                    then(V.tensor_reduce(w_gat2[:, 32 + s:33 + s], a_gat2[:, s, :], AX.X, ALU.add))

            def edge_pass(k, meanwhile=None):
                w = RUN_W[k]
                tables_stored(v, k)
                for b in range(NB):
                    hand_indices(k, b, b)
                if meanwhile:
                    meanwhile()
                zero_tail = run_view(NB - 1, w)[:, C - 1, :]
                then(V.memset(zero_tail, 0.0))
                if k in HEADS:
                    then(V.memset(zero_tail[:, w - HEADS[k]:w], -BIG))
                if k in SPREAD:
                    v.wait_ge(s_first, 16 * (SPREAD_NO[k] + 1))
                    then(V.tensor_copy(carry[:, 0:SPREAD[k]], first_row[:, SPREAD_AT[k]:SPREAD_AT[k] + SPREAD[k]]))
                with v.Fori(0, NIT) as i:
                    fresh()
                    for b in range(NB):
                        edge_chunk(k, i, b)

            V.memset(w_heads[:, :], 0.0)
            V.memset(w_refl2[:, :], 0.0)
            V.memset(w_refl1[:, :, :], 0.0)
            V.memset(x[:, NT - 1, :], 0.0)
            V.memset(scratch[:, SCRATCH - P:SCRATCH], 0.0)
            then(V.memset(ends[:, 0:(EDGES + P) // P], 0.0))
            v.sem_inc(s_zero_src, 1)
            V.memset(ones[:, :], 1.0)
            V.memset(same_c[:, :], 0.0)
            V.memset(row_of_src[:, COLS:COLS + NB * C], 0)
            V.memset(etype[:, COLS:COLS + NB * C], 0.0)
            v.wait_ge(s_iota, 2)
            V.tensor_copy(iota_bf[:, :], iota_row[:, :])
            ts(ident[:, :], iota_row[:, :], iota_p[:, 0:1], None, ALU.is_equal)
            ts(upto[:, :], iota_row[:, :], iota_p[:, 0:1], None, ALU.is_ge)
            ts(below[:, :], iota_row[:, :], iota_p[:, 0:1], None, ALU.is_lt)
            ts(spare_edge[:, :], iota_p[:, :], float(EDGES), None, ALU.add)
            then(ts(spare_node[:, :], iota_p[:, :], float(ROWS), None, ALU.add))
            v.wait_ge(s_dst, 16 * N_LOADS_DST)
            raw = work[:, :].bitcast(I32)
            dst_raw, src_raw, type_raw = raw[:, 0:COLS], raw[:, COLS:2 * COLS], raw[:, 2 * COLS:3 * COLS]
            low_tmp = raw[:, 3 * COLS:4 * COLS]
            split = lambda o, a, op, n: V.tensor_single_scalar(o, a, n, op)

            def low_high(ids, n):
                then(split(low_tmp[:, 0:n], ids, ALU.bitwise_and, P - 1))
                then(V.tensor_copy(lo_all[:, 0:n], low_tmp[:, 0:n]))
                then(split(low_tmp[:, 0:n], ids, ALU.logical_shift_right, 7))
                then(V.tensor_copy(hi_all[:, 0:n], low_tmp[:, 0:n]))

            low_high(dst_raw.rearrange("p (s w) -> p s w", w=BLK)[:, :, BLK - 1], SAMPLES)
            v.sem_inc(s_hist_zero, 1)
            fresh()
            with v.Fori(0, SAMPLES // C) as i:
                count_step(i, 0)
            v.wait_ge(s_hist_done, 1)
            then(V.tensor_copy(small[:, 0, :], ps_hist[:, 0:NT]))
            ask_pe(2)
            then(V.tensor_copy(small[:, 1, :], ps_misc[:, P:P + NT]))
            then(V.tensor_tensor_scan(small[:, 2, :], ones[:, 0:NT], small[:, 1, :], 0.0, ALU.mult, ALU.add))
            then(tt(small[:, 2, :], small[:, 2, :], small[:, 1, :], ALU.subtract))
            then(tt(has[:, :], ps_misc[:, 0:NT], small[:, 2, :], ALU.add))
            then(ts(has[:, :], has[:, :], float(BLOCKS - 1), None, ALU.min))
            then(V.tensor_copy(block_idx[:, :], has[:, :]))
            v.sem_inc(s_block_idx, 1)
            v.wait_ge(s_loads, 16 * N_LOADS)
            V.tensor_copy(etype[:, 0:COLS], type_raw)
            V.memset(same[:, 0:1], 1.0)
            tt(same[:, 1:COLS], dst_raw[:, 1:COLS], dst_raw[:, 0:COLS - 1], ALU.is_equal)
            low_high(src_raw, COLS)
            then(V.scalar_tensor_tensor(row_of_src[:, 0:COLS], lo_all, float(NT), hi_all, ALU.mult, ALU.add))
            v.sem_inc(s_hist_zero, 1)
            ts(next_of, iota_row[:, :], iota_p[:, 0:1], 1.0, ALU.subtract, ALU.is_equal)
            ts(first_of_last, iota_row[:, :], iota_p[:, 0:1], 1.0 - P, ALU.subtract, ALU.is_equal)
            layer_norm()
            node_id = small[:, 1, :]
            then(ts(node_id, iota_row[:, 0:NT], float(P), iota_p[:, 0:1], ALU.mult, ALU.add))
            v.wait_ge(s_blocks, N_ENDS)
            then(V.tensor_copy(block_f, block_dst))
            then(tt(block_le, block_f, bc_last(node_id, BLK), ALU.is_le))
            then(V.tensor_reduce(small[:, 2, :], block_le, AX.X, ALU.add))
            upto_node, upto_last = small[:, 2, :], small[:, 3, :]
            then(V.scalar_tensor_tensor(upto_node, has[:, :], float(BLK), upto_node, ALU.mult, ALU.add))
            V.memset(upto_last[:, 0:1], 0.0)
            then(V.tensor_copy(upto_last[:, 1:NT], upto_node[:, 0:NT - 1]))
            ask_pe(2)
            then(tt(cnt[:, :], upto_node, ps_misc[:, 0:NT], ALU.subtract))
            then(tt(cnt[:, :], cnt[:, :], ps_misc[:, P:P + NT], ALU.subtract))
            then(ts(small[:, 0, :], cnt[:, :], 1.0, None, ALU.add))
            tell_act()
            then(ts(dis[:, :], upto_node, -1.0, 0.0, ALU.add, ALU.max))
            V.tensor_copy(end_idx[:, :], dis[:, :])
            then(ts(has[:, :], cnt[:, :], 0.5, None, ALU.is_gt))
            then(tt(small[:, 3, :], upto_node, cnt[:, :], ALU.subtract))
            then(ts(small[:, 3, :], small[:, 3, :], spare_edge[:, 0:1], None, ALU.subtract))
            then(tt(small[:, 3, :], small[:, 3, :], has[:, :], ALU.mult))
            then(ts(start_idx[:, :], small[:, 3, :], spare_edge[:, 0:1], None, ALU.add))
            hear_act()
            then(V.reciprocal(dinv[:, :], small[:, 1, :]))
            rows16 = nodes(node_rows, 16)
            then(tt(rows16, hn[:, :, :], bc_last(dinv[:, :], 16), ALU.mult))
            v.sem_inc(s_rows_ready, 1)
            edge_pass(GCN1, boundaries)
            total = summed(GCN1)
            then(ts(inv_count[:, :, :], total[:, :, 16:24], 1.0, None, ALU.max))
            then(V.reciprocal(inv_count[:, :, :], inv_count[:, :, :]))
            v.sem_inc(s_rows_ready, 1)
            v.wait_ge(s_hist_done, 2)
            then(tt(cnt[:, :], cnt[:, :], ps_hist[:, 0:NT], ALU.add))
            agg = total[:, :, 0:16]
            then(tt(agg, agg, rows16, ALU.add))
            then(tt(agg, agg, bc_last(dinv[:, :], 16), ALU.mult))
            hid = nodes(work, 32)
            linear(hid, agg, 16, 32, b_gcn1)
            then(ts(hid, hid, 0.0, None, ALU.max))
            linear(rows16, hid, 32, 16)
            then(tt(rows16, rows16, bc_last(dinv[:, :], 16), ALU.mult))
            v.sem_inc(s_rows_ready, 1)
            edge_pass(GCN2)
            total = summed(GCN2)
            then(tt(total, total, rows16, ALU.add))
            then(tt(total, total, bc_last(dinv[:, :], 16), ALU.mult))
            then(tt(total, total, bc_mid(b_gcn2, NT), ALU.add))
            then(tt(x[:, :, :], x[:, :, :], total, ALU.add))

            layer_norm()
            rows_gat1 = nodes(node_rows, 22)
            then(V.tensor_copy(rows_gat1[:, :, 0:16], hn[:, :, :]))
            linear(rows_gat1[:, :, 16:22], hn[:, :, :], 16, 6)
            v.sem_inc(s_rows_ready, 1)
            edge_pass(GAT1)
            agg = gat_nodes(GAT1)
            hid = nodes(work, 96)
            v.wait_ge(s_blk, 16 * 21)
            linear(hid, agg, 48, 96, b_gat1)
            for half in range(2):
                selu(hid[:, :, 48 * half:48 * half + 48], 48)
            rows_gat2 = nodes(node_rows, 34)
            linear(rows_gat2, hid, 96, 34)
            v.sem_inc(s_rows_ready, 1)
            edge_pass(GAT2)
            agg = gat_nodes(GAT2)
            then(tt(agg, agg, bc_mid(b_gat2, NT), ALU.add))
            selu(agg, 32)
            fin = nodes(work, 16)
            linear(fin, agg, 32, 16, b_fin)
            then(tt(x[:, :, :], x[:, :, :], fin, ALU.add))

            layer_norm()
            then(ts(small[:, 0, :], cnt[:, :], 1e-5, None, ALU.max))
            inverse_sqrt(dis[:, :])
            rows_sheaf = nodes(node_rows, 17)
            V.tensor_copy(rows_sheaf[:, :, 0:16], hn[:, :, :])
            then(V.tensor_copy(rows_sheaf[:, :, 16], dis[:, :]))
            v.sem_inc(s_rows_ready, 1)
            edge_pass(SHEAF)
            pass_done(SHEAF)
            v.sem_inc(s_acc_go, 1)
            more = extras(16)
            part = nodes(scratch, 16, NT * 16)
            for n, m in enumerate(ACC_LOADS):
                v.wait_ge(s_acc_in[n % 2], 16 * sum(ACC_LOADS[n % 2:n + 1:2]))
                o = (n % 2) * 4 * NT * 16
                then(V.tensor_reduce(part, work[:, o:o + m * NT * 16].rearrange("p (m t f) -> p t f m", m=m, f=16), AX.X, ALU.add))
                v.sem_inc(s_acc_used, 1)
                then(tt(more, more, part, ALU.add))
            total = ends_in(SHEAF)
            then(tt(total, total, bc_last(has[:, :], 16), ALU.mult))
            then(tt(total, total, more, ALU.add))
            then(tt(total, total, bc_last(dis[:, :], 16), ALU.mult))
            then(tt(total, total, hn[:, :, :], ALU.add))
            then(ts(total, total, 0.0, None, ALU.max))
            then(tt(x[:, :, :], x[:, :, :], total, ALU.add))

            layer_norm()
            for half in range(2):
                linear(nodes(work, P), hn[:, :, :], 16, P, relations=half)
            root1 = nodes(node_rows, 32)
            edge_pass(REL1, lambda: linear(root1, hn[:, :, :], 16, 32, b_rel1))
            total = summed(REL1)
            then(tt(total, total, root1, ALU.add))
            hid = total
            then(ts(hid, hid, 0.0, None, ALU.max))
            linear(nodes(work, P), hid, 32, P, relations=2)
            root2 = nodes(node_rows, 16)
            edge_pass(REL2, lambda: linear(root2, hid, 32, 16, b_rel2))
            total = summed(REL2)
            then(tt(total, total, root2, ALU.add))
            then(tt(x[:, :, :], x[:, :, :], total, ALU.add))
            v.sem_inc(s_final, 1)


_INS = ['x', 'src', 'dst', 'edge_type_8', 'L0_gnn_W1', 'L0_gnn_b1', 'L0_gnn_W2', 'L0_gnn_b2', 'L1_gnn_W1', 'L1_gnn_a_src1',
        'L1_gnn_a_dst1', 'L1_gnn_b1', 'L1_gnn_W2', 'L1_gnn_a_src2', 'L1_gnn_a_dst2', 'L1_gnn_b2', 'L1_gnn_Wf', 'L1_gnn_bf',
        'L2_gnn_W1', 'L2_gnn_b1', 'L2_gnn_W2', 'L2_gnn_b2', 'L3_gnn_W1', 'L3_gnn_root1', 'L3_gnn_b1', 'L3_gnn_W2',
        'L3_gnn_root2', 'L3_gnn_b2']


def kernel(**inputs):
    import numpy as _np
    import concourse.bacc as _bacc
    from concourse import mybir as _mybir
    from concourse.bass_utils import run_bass_kernel_spmd as _run

    nc = _bacc.Bacc("TRN2", target_bir_lowering=False, num_devices=1)
    arrays, args = {}, {}
    for name in _INS:
        a = _np.asarray(inputs[name])
        if name in ("L2_gnn_W1", "L2_gnn_W2"):
            a = a.T
        if name in ("L3_gnn_W1", "L3_gnn_W2"):
            a = a.transpose(1, 0, 2).reshape(a.shape[1], -1)
        a = _np.ascontiguousarray(a)
        arrays[f"in_{name}"] = a
        args[name] = nc.dram_tensor(f"in_{name}", a.shape, _mybir.dt.from_np(a.dtype), kind="ExternalInput").ap()
    out = nc.dram_tensor("out_x", (NODES, 16), _mybir.dt.float32, kind="ExternalOutput").ap()
    build_kernel(nc, args, out)
    r = _run(nc, [arrays], core_ids=[0])
    return r.results[0]["out_x"]
```
